# Optimizing a Trainium2 kernel written in Bass

```python
import numpy as np
import jax
import jax.numpy as jnp

def _softmax(x, axis=-1):
    return jax.nn.softmax(x, axis=axis)

def _gelu(x):
    return jax.nn.gelu(x, approximate=True)

def _silu(x):
    return jax.nn.silu(x)

def _sigmoid(x):
    return jax.nn.sigmoid(x)

def _layernorm(x, axis=-1, eps=1e-05):
    m = jnp.mean(x, axis=axis, keepdims=True)
    v = jnp.var(x, axis=axis, keepdims=True)
    return (x - m) / jnp.sqrt(v + eps)

def _scatter_add(tgt, idx, src, axis=0):
    return tgt.at[idx].add(src)

def _segment_sum(src, seg, n):
    return jax.ops.segment_sum(src, seg, n)
kernel_name = 'mk_dlrm_tower_d1_rec_r8_adbe32'

def setup_inputs(seed: int=0):
    np.random.seed(seed)
    _w = jnp.asarray

    def _rec_inputs():
        import jax
        import jax.numpy as jnp
        _tk = jax.random.key(seed)
        dense_ctx = jax.random.normal(jax.random.fold_in(_tk, 190), (512, 16), jnp.float32)
        ids = jnp.stack([jax.random.randint(jax.random.fold_in(_tk, 200 + f), (512,), 0, v, jnp.int32) for f, v in enumerate([125000, 125000, 1250, 125000, 1250, 1250, 1000, 1250, 1000, 12500, 1250, 125000, 1000, 125000, 125000, 125000, 1000, 1000, 12500, 1000, 1250, 1000, 1000, 1000, 1000, 1000, 1250, 12500, 1250, 1000, 1000, 1250])], axis=1)
        tbl_0 = 0.05 * jax.random.normal(jax.random.fold_in(_tk, 500 + 0), (125000, 32), jnp.float32)
        tbl_1 = 0.05 * jax.random.normal(jax.random.fold_in(_tk, 500 + 1), (125000, 32), jnp.float32)
        tbl_2 = 0.05 * jax.random.normal(jax.random.fold_in(_tk, 500 + 2), (1250, 32), jnp.float32)
        tbl_3 = 0.05 * jax.random.normal(jax.random.fold_in(_tk, 500 + 3), (125000, 32), jnp.float32)
        tbl_4 = 0.05 * jax.random.normal(jax.random.fold_in(_tk, 500 + 4), (1250, 32), jnp.float32)
        tbl_5 = 0.05 * jax.random.normal(jax.random.fold_in(_tk, 500 + 5), (1250, 32), jnp.float32)
        tbl_6 = 0.05 * jax.random.normal(jax.random.fold_in(_tk, 500 + 6), (1000, 32), jnp.float32)
        tbl_7 = 0.05 * jax.random.normal(jax.random.fold_in(_tk, 500 + 7), (1250, 32), jnp.float32)
        tbl_8 = 0.05 * jax.random.normal(jax.random.fold_in(_tk, 500 + 8), (1000, 32), jnp.float32)
        tbl_9 = 0.05 * jax.random.normal(jax.random.fold_in(_tk, 500 + 9), (12500, 32), jnp.float32)
        tbl_10 = 0.05 * jax.random.normal(jax.random.fold_in(_tk, 500 + 10), (1250, 32), jnp.float32)
        tbl_11 = 0.05 * jax.random.normal(jax.random.fold_in(_tk, 500 + 11), (125000, 32), jnp.float32)
        tbl_12 = 0.05 * jax.random.normal(jax.random.fold_in(_tk, 500 + 12), (1000, 32), jnp.float32)
        tbl_13 = 0.05 * jax.random.normal(jax.random.fold_in(_tk, 500 + 13), (125000, 32), jnp.float32)
        tbl_14 = 0.05 * jax.random.normal(jax.random.fold_in(_tk, 500 + 14), (125000, 32), jnp.float32)
        tbl_15 = 0.05 * jax.random.normal(jax.random.fold_in(_tk, 500 + 15), (125000, 32), jnp.float32)
        tbl_16 = 0.05 * jax.random.normal(jax.random.fold_in(_tk, 500 + 16), (1000, 32), jnp.float32)
        tbl_17 = 0.05 * jax.random.normal(jax.random.fold_in(_tk, 500 + 17), (1000, 32), jnp.float32)
        tbl_18 = 0.05 * jax.random.normal(jax.random.fold_in(_tk, 500 + 18), (12500, 32), jnp.float32)
        tbl_19 = 0.05 * jax.random.normal(jax.random.fold_in(_tk, 500 + 19), (1000, 32), jnp.float32)
        tbl_20 = 0.05 * jax.random.normal(jax.random.fold_in(_tk, 500 + 20), (1250, 32), jnp.float32)
        tbl_21 = 0.05 * jax.random.normal(jax.random.fold_in(_tk, 500 + 21), (1000, 32), jnp.float32)
        tbl_22 = 0.05 * jax.random.normal(jax.random.fold_in(_tk, 500 + 22), (1000, 32), jnp.float32)
        tbl_23 = 0.05 * jax.random.normal(jax.random.fold_in(_tk, 500 + 23), (1000, 32), jnp.float32)
        tbl_24 = 0.05 * jax.random.normal(jax.random.fold_in(_tk, 500 + 24), (1000, 32), jnp.float32)
        tbl_25 = 0.05 * jax.random.normal(jax.random.fold_in(_tk, 500 + 25), (1000, 32), jnp.float32)
        tbl_26 = 0.05 * jax.random.normal(jax.random.fold_in(_tk, 500 + 26), (1250, 32), jnp.float32)
        tbl_27 = 0.05 * jax.random.normal(jax.random.fold_in(_tk, 500 + 27), (12500, 32), jnp.float32)
        tbl_28 = 0.05 * jax.random.normal(jax.random.fold_in(_tk, 500 + 28), (1250, 32), jnp.float32)
        tbl_29 = 0.05 * jax.random.normal(jax.random.fold_in(_tk, 500 + 29), (1000, 32), jnp.float32)
        tbl_30 = 0.05 * jax.random.normal(jax.random.fold_in(_tk, 500 + 30), (1000, 32), jnp.float32)
        tbl_31 = 0.05 * jax.random.normal(jax.random.fold_in(_tk, 500 + 31), (1250, 32), jnp.float32)
        _rk = jax.random.fold_in(_tk, 7)
        W_top1 = 0.0606339 * jax.random.normal(jax.random.fold_in(_tk, 801), (272, 512), jnp.float32)
        W_top2 = 0.0441942 * jax.random.normal(jax.random.fold_in(_tk, 802), (512, 256), jnp.float32)
        W_top3 = 0.0625 * jax.random.normal(jax.random.fold_in(_tk, 803), (256, 1), jnp.float32)
        b_top1 = jnp.zeros((512,), jnp.float32)
        b_top2 = jnp.zeros((256,), jnp.float32)
        return (dense_ctx, ids, tbl_0, tbl_1, tbl_2, tbl_3, tbl_4, tbl_5, tbl_6, tbl_7, tbl_8, tbl_9, tbl_10, tbl_11, tbl_12, tbl_13, tbl_14, tbl_15, tbl_16, tbl_17, tbl_18, tbl_19, tbl_20, tbl_21, tbl_22, tbl_23, tbl_24, tbl_25, tbl_26, tbl_27, tbl_28, tbl_29, tbl_30, tbl_31, W_top1, b_top1, W_top2, b_top2, W_top3)
    dense_ctx, ids, tbl_0, tbl_1, tbl_2, tbl_3, tbl_4, tbl_5, tbl_6, tbl_7, tbl_8, tbl_9, tbl_10, tbl_11, tbl_12, tbl_13, tbl_14, tbl_15, tbl_16, tbl_17, tbl_18, tbl_19, tbl_20, tbl_21, tbl_22, tbl_23, tbl_24, tbl_25, tbl_26, tbl_27, tbl_28, tbl_29, tbl_30, tbl_31, W_top1, b_top1, W_top2, b_top2, W_top3 = _rec_inputs()

    def _L0_rec_setup():
        import jax, jax.numpy as jnp
        import numpy as np
        B, N, K = (256, 32, 32)
        CIN_SIZE = [128, 128]
        key = jax.random.key(seed)
        k1, k2, k3 = jax.random.split(key, 3)
        inputs = jax.random.normal(k1, (B, N, K), dtype=jnp.float32)
        W0 = jax.random.normal(k2, (N * N, CIN_SIZE[0]), dtype=jnp.float32) * 0.04
        W1 = jax.random.normal(k3, (N * CIN_SIZE[0], CIN_SIZE[1]), dtype=jnp.float32) * 0.02
        return {'inputs': inputs, 'W0': W0, 'W1': W1}
    _L0_rec_all = _L0_rec_setup()
    _L0_rec_in = {k: v for k, v in _L0_rec_all.items() if k in ('W0', 'W1')}
    del _L0_rec_all
    return {'dense_ctx': dense_ctx, 'ids': ids, 'tbl_0': tbl_0, 'tbl_1': tbl_1, 'tbl_2': tbl_2, 'tbl_3': tbl_3, 'tbl_4': tbl_4, 'tbl_5': tbl_5, 'tbl_6': tbl_6, 'tbl_7': tbl_7, 'tbl_8': tbl_8, 'tbl_9': tbl_9, 'tbl_10': tbl_10, 'tbl_11': tbl_11, 'tbl_12': tbl_12, 'tbl_13': tbl_13, 'tbl_14': tbl_14, 'tbl_15': tbl_15, 'tbl_16': tbl_16, 'tbl_17': tbl_17, 'tbl_18': tbl_18, 'tbl_19': tbl_19, 'tbl_20': tbl_20, 'tbl_21': tbl_21, 'tbl_22': tbl_22, 'tbl_23': tbl_23, 'tbl_24': tbl_24, 'tbl_25': tbl_25, 'tbl_26': tbl_26, 'tbl_27': tbl_27, 'tbl_28': tbl_28, 'tbl_29': tbl_29, 'tbl_30': tbl_30, 'tbl_31': tbl_31, 'W_top1': W_top1, 'b_top1': b_top1, 'W_top2': W_top2, 'b_top2': b_top2, 'W_top3': W_top3, 'L0_rec_W0': _L0_rec_in['W0'], 'L0_rec_W1': _L0_rec_in['W1']}

def reference(dense_ctx, ids, tbl_0, tbl_1, tbl_2, tbl_3, tbl_4, tbl_5, tbl_6, tbl_7, tbl_8, tbl_9, tbl_10, tbl_11, tbl_12, tbl_13, tbl_14, tbl_15, tbl_16, tbl_17, tbl_18, tbl_19, tbl_20, tbl_21, tbl_22, tbl_23, tbl_24, tbl_25, tbl_26, tbl_27, tbl_28, tbl_29, tbl_30, tbl_31, W_top1, b_top1, W_top2, b_top2, W_top3, L0_rec_W0, L0_rec_W1):
    import jax
    import jax.numpy as jnp

    def _L0_rec_ref(inputs, W0, W1):
        import jax, jax.numpy as jnp
        import numpy as np
        B, N, K = (256, 32, 32)
        CIN_SIZE = [128, 128]
        b, n, k = inputs.shape
        x = inputs
        res = []
        for W in (W0, W1):
            prev = x.shape[1]
            z = jnp.einsum('bhd,bmd->bhmd', inputs, x).reshape(b, n * prev, k)
            x = jnp.einsum('bpd,pj->bjd', z, W)
            res.append(x)
        out = jnp.sum(jnp.concatenate(res, axis=1), axis=-1)
        return out
    e = jnp.stack([tbl_0[ids[:, 0]], tbl_1[ids[:, 1]], tbl_2[ids[:, 2]], tbl_3[ids[:, 3]], tbl_4[ids[:, 4]], tbl_5[ids[:, 5]], tbl_6[ids[:, 6]], tbl_7[ids[:, 7]], tbl_8[ids[:, 8]], tbl_9[ids[:, 9]], tbl_10[ids[:, 10]], tbl_11[ids[:, 11]], tbl_12[ids[:, 12]], tbl_13[ids[:, 13]], tbl_14[ids[:, 14]], tbl_15[ids[:, 15]], tbl_16[ids[:, 16]], tbl_17[ids[:, 17]], tbl_18[ids[:, 18]], tbl_19[ids[:, 19]], tbl_20[ids[:, 20]], tbl_21[ids[:, 21]], tbl_22[ids[:, 22]], tbl_23[ids[:, 23]], tbl_24[ids[:, 24]], tbl_25[ids[:, 25]], tbl_26[ids[:, 26]], tbl_27[ids[:, 27]], tbl_28[ids[:, 28]], tbl_29[ids[:, 29]], tbl_30[ids[:, 30]], tbl_31[ids[:, 31]]], axis=1)
    z = _L0_rec_ref(e, L0_rec_W0, L0_rec_W1)
    z = z.reshape(z.shape[0], -1)
    h = jnp.concatenate([z, dense_ctx], axis=1)
    h = jnp.maximum(h @ W_top1 + b_top1, 0.0)
    h = jnp.maximum(h @ W_top2 + b_top2, 0.0)
    y = h @ W_top3
    return y

_drawn_inputs = setup_inputs


def setup_inputs(seed=0):
    import zlib

    import numpy as np

    out = dict(_drawn_inputs(seed))
    spreads = {'b_top1': (0.0, 0.1), 'b_top2': (0.0, 0.1)}
    factors = {'tbl_0': 4.855,
     'tbl_1': 4.621,
     'tbl_2': 5.016,
     'tbl_3': 5.376,
     'tbl_4': 5.011,
     'tbl_5': 5.263,
     'tbl_6': 5.526,
     'tbl_7': 4.983,
     'tbl_8': 5.06,
     'tbl_9': 4.794,
     'tbl_10': 5.048,
     'tbl_11': 5.294,
     'tbl_12': 4.888,
     'tbl_13': 4.753,
     'tbl_14': 5.125,
     'tbl_15': 4.865,
     'tbl_16': 4.99,
     'tbl_17': 5.477,
     'tbl_18': 5.327,
     'tbl_19': 5.366,
     'tbl_20': 4.805,
     'tbl_21': 4.734,
     'tbl_22': 5.152,
     'tbl_23': 4.987,
     'tbl_24': 4.894,
     'tbl_25': 4.683,
     'tbl_26': 4.655,
     'tbl_27': 4.846,
     'tbl_28': 5.135,
     'tbl_29': 4.884,
     'tbl_30': 4.705,
     'tbl_31': 4.366,
     'L0_rec_W1': 8.0}
    for name, (base, spread) in spreads.items():
        noise = np.random.default_rng([zlib.crc32(name.encode()), seed]).standard_normal(out[name].shape)
        drawn = base * np.exp(spread * noise) if base else spread * noise
        out[name] = jnp.asarray(drawn.astype(out[name].dtype))
    for name, factor in factors.items():
        out[name] = (out[name] * factor).astype(out[name].dtype)
    return out
```

```python
from contextlib import ExitStack

import concourse.bass as bass
from concourse import mybir

FP32 = mybir.dt.float32
INT32 = mybir.dt.int32
ALU = mybir.AluOpType
ACT = mybir.ActivationFunctionType

P = 128
B, F, D = 512, 32, 32
J = 128
CTX = 16
N1, N2 = 512, 256
T = B // P
Q = P // D
G = P // Q
HALF = F // 2
S = HALF // 2
PAIRS = HALF * (HALF - 1) // 2
ROW = S * HALF
WRAP = HALF + S
CROSS = HALF * HALF
FW = CROSS + F
BANK = 512
QUAD = BANK // P
NQ = G // QUAD
F8 = F // Q
HPB = BANK // J
M1, M2 = N1 // P, N2 // P


def build(nc, dense_ctx, ids, tables, w_top1, b_top1, w_top2, b_top2, w_top3, w0, w1, out):
    with ExitStack() as ctx:
        def sbuf(name, shape, dt=FP32):
            return ctx.enter_context(nc.sbuf_tensor(name, shape, dt))

        def sem(name):
            return ctx.enter_context(nc.semaphore(name))

        idx = sbuf("idx", [P, T, F], INT32)
        rows = sbuf("rows", [P, F * D])
        fields = sbuf("fields", [P, 2, WRAP, G])
        diag_blocks = sbuf("diag_blocks", [P, G, Q, F])
        pairs = sbuf("pairs", [P, G, 2, ROW])
        squares = sbuf("squares", [P, G * 2 * F])
        squares_v = squares[:, :].rearrange("p (g k f) -> p g k f", g=G, k=2)
        sums = sbuf("sums", [P, 2 * F * P + 2 * F8 * P + F * P])
        at = 2 * F * P
        tri = sums[:, 0:at].rearrange("p (c h x) -> p c h x", c=2, h=F)
        packed = sums[:, at:at + 2 * F8 * P].rearrange("p (k f x) -> p k f x", k=2, f=F8)
        at += 2 * F8 * P
        wide = sums[0:2 * F, at:at + F * P].rearrange("p (h x) -> p h x", h=F)
        moved = sums[:, at:at + F * P].rearrange("p (c h r) -> p c h r", c=2, h=HALF)
        left = sums[:, 0:F * FW].rearrange("p (h w) -> p h w", h=F)
        sq_cols = sums[:, F * FW:F * FW + F8 * P].rearrange("p (f r) -> p f r", f=F8)
        w1_sb = sbuf("w1_sb", [P, F, J])
        w0_sb = sbuf("w0_sb", [P, F8, J])
        w0_t = squares[:, 0:F * F].rearrange("p (a c) -> p a c", a=F)
        w0_wrap = squares[:, F * F:F * F + F * WRAP].rearrange("p (k a c) -> p k a c", k=2, a=HALF)
        w_pair = sbuf("w_pair", [P, 2, ROW])
        w_cross = sbuf("w_cross", [P, FW])
        v_pair = sbuf("v_pair", [P, 2, F, J])
        v_square = sbuf("v_square", [P, F8, J])
        ident = sbuf("ident", [P, P])
        top1 = sbuf("top1", [P, 2, N1])
        top1_ctx = sbuf("top1_ctx", [CTX, N1])
        top2 = sbuf("top2", [P, M1, N2])
        top3 = sbuf("top3", [P, M2])
        bias1 = sbuf("bias1", [P, M1])
        bias2 = sbuf("bias2", [P, M2])
        dense = sbuf("dense", [P, T, CTX])
        dense_t = sbuf("dense_t", [CTX, T, P])
        inter = sbuf("inter", [P, 2, P])
        hid1 = sbuf("hid1", [P, M1, P])
        hid2 = sbuf("hid2", [P, M2, P])
        y_row = sbuf("y_row", [1, B])

        psum = ctx.enter_context(nc.psum_tensor("psum", [P, 8, BANK], FP32))
        quad_banks = [[psum[:, 2 * kind + n, :].rearrange("p (x h) -> p h x", h=F) for n in range(2)]
                      for kind in range(3)]
        ps_x = psum[:, 6, 0:2 * P].rearrange("p (k x) -> p k x", k=2)
        ps_h2 = psum[:, 6, 2 * P:4 * P].rearrange("p (m x) -> p m x", m=M2)
        ps_h1 = psum[:, 7, :].rearrange("p (m x) -> p m x", m=M1)
        ps_y = psum[0:1, 7, 0:P]

        ids_loaded = sem("ids_loaded")
        w0_loaded = sem("w0_loaded")
        w1_loaded = sem("w1_loaded")
        tower_loaded = sem("tower_loaded")
        ident_cleared = sem("ident_cleared")
        ident_ready = sem("ident_ready")
        blocks_cleared = sem("blocks_cleared")
        gathered = sem("gathered")
        rows_turned = sem("rows_turned")
        fields_ready = sem("fields_ready")
        blocks_ready = sem("blocks_ready")
        pairs_ready = sem("pairs_ready")
        squares_ready = sem("squares_ready")
        w0_turned = sem("w0_turned")
        w0_t_saved = sem("w0_t_saved")
        dense_turned = sem("dense_turned")
        dense_saved = sem("dense_saved")
        w0_wrapped = sem("w0_wrapped")
        w_cross_ready = sem("w_cross_ready")
        w_pair_ready = sem("w_pair_ready")
        left_formed = sem("left_formed")
        left_saved = sem("left_saved")
        moved_ready = sem("moved_ready")
        squares_copied = sem("squares_copied")
        sq_cols_ready = sem("sq_cols_ready")
        v_formed = sem("v_formed")
        v_saved = sem("v_saved")
        quad_formed = sem("quad_formed")
        quad_saved_act = sem("quad_saved_act")
        quad_saved_dve = sem("quad_saved_dve")
        wide_packed = sem("wide_packed")
        x_summed = sem("x_summed")
        x_saved = sem("x_saved")
        h1_summed = sem("h1_summed")
        h1_ready = sem("h1_ready")
        h2_summed = sem("h2_summed")
        h2_ready = sem("h2_ready")
        y_summed = sem("y_summed")
        y_saved = sem("y_saved")
        y_stored = sem("y_stored")
        block = ctx.enter_context(nc.Block())

        NV = 2 * F // HPB + 2
        PACKS = 16 * 2 * Q

        def v_order(k):
            n = HALF // HPB
            step, k = divmod(k, 2 * n)
            half, k = divmod(k, n)
            return half, ((half + step) % 2) * HALF + k * HPB

        @block.sync
        def _(sp):
            sp.dma_start(idx[:, :, :], ids.rearrange("(t p) f -> p t f", p=P)).then_inc(ids_loaded, 16)
            w0_v = w0.rearrange("(r f c) j -> r c f j", r=Q, f=F8)
            for r in range(Q):
                sp.dma_start(w0_sb[r * F:(r + 1) * F, :, :], w0_v[r]).then_inc(w0_loaded, 16)
            sp.dma_start(w1_sb[:, :, :], w1.rearrange("(h m) j -> m h j", m=J)).then_inc(w1_loaded, 16)
            with nc.allow_non_contiguous_dma(reason="a few hundred biases"):
                for dst, src in (
                    (dense[:, :, :], dense_ctx.rearrange("(t p) c -> p t c", p=P)),
                    (top1[:, :, :], w_top1[0:2 * J, :].rearrange("(k p) n -> p k n", p=P)),
                    (top1_ctx[:, :], w_top1[2 * J:2 * J + CTX, :]),
                    (top2[:, :, :], w_top2.rearrange("(k p) n -> p k n", p=P)),
                    (top3[:, :], w_top3.rearrange("(k p) n -> p (k n)", p=P)),
                    (bias1[:, :], b_top1.rearrange("(k p) -> p k", p=P)),
                    (bias2[:, :], b_top2.rearrange("(k p) -> p k", p=P)),
                ):
                    sp.dma_start(dst, src).then_inc(tower_loaded, 16)

            with sp.Fori(0, T) as t:
                sp.wait_ge(quad_saved_act, t * NQ + NQ)
                for kind in range(2):
                    for r in range(Q):
                        sp.dma_start(packed[r * F:(r + 1) * F, kind, :, :],
                                     wide[kind * F:(kind + 1) * F, r * F8:(r + 1) * F8, :]
                                     ).then_inc(wide_packed, 16)
            sp.wait_ge(y_saved, T)
            sp.dma_start(out.rearrange("b o -> o b"), y_row[:, :]).then_inc(y_stored, 16)
            sp.wait_ge(y_stored, 16)

        @block.gpsimd
        def _(pool):
            nc.gpsimd.memset(ident[:, :], 0.0).then_inc(ident_cleared, 1)
            pool.wait_ge(ident_cleared, 1)
            nc.gpsimd.affine_select(out=ident[:, :], in_=ident[:, :], compare_op=ALU.not_equal, fill=1.0,
                                    base=0, pattern=[[-1, P]], channel_multiplier=1).then_inc(ident_ready, 1)
            pool.wait_ge(ids_loaded, 16)
            for t in range(T):
                if t:
                    pool.wait_ge(rows_turned, t)
                for f in range(F):
                    pool.indirect_dma_start(rows[:, f * D:(f + 1) * D], None, tables[f],
                                            bass.IndirectOffsetOnAxis(idx[:, t, f:f + 1], 0)
                                            ).then_inc(gathered, 16)

        @block.vector
        def _(dve):
            nc.vector.memset(diag_blocks[:, :, :, :], 0.0).then_inc(blocks_cleared, 1)

            dve.wait_ge(w0_t_saved, 1)
            swapped = w0_t.rearrange("p a c -> p c a")
            nc.vector.tensor_tensor(
                w_cross[:, 0:CROSS].rearrange("p (a c) -> p a c", a=HALF),
                w0_t[:, 0:HALF, HALF:F], swapped[:, 0:HALF, HALF:F], ALU.add)
            nc.vector.tensor_copy(w_cross[:, CROSS:FW], squares[:, 0:F * F:F + 1]).then_inc(w_cross_ready, 1)
            for half in range(2):
                own = slice(half * HALF, (half + 1) * HALF)
                first = slice(half * HALF, half * HALF + S)
                nc.vector.tensor_tensor(w0_wrap[:, half, :, 0:HALF], w0_t[:, own, own], swapped[:, own, own],
                                        ALU.add)
                last = nc.vector.tensor_tensor(w0_wrap[:, half, :, HALF:WRAP], w0_t[:, own, first],
                                               swapped[:, own, first], ALU.add)
            last.then_inc(w0_wrapped, 1)
            dve.wait_ge(w0_wrapped, 1)
            for half in range(2):
                for s in range(1, S + 1):
                    start = F * F + half * HALF * WRAP + s
                    last = nc.vector.tensor_copy(w_pair[:, half, (s - 1) * HALF:s * HALF],
                                                 squares[:, start:start + (HALF - 1) * (WRAP + 1) + 1:WRAP + 1])
            last.then_inc(w_pair_ready, 1)

            dve.wait_ge(left_saved, F // 2)
            for half in range(2):
                other, third = (HALF, 1) if half == 0 else (1, HALF)
                base = half * HALF * FW

                def products(i, k, n):
                    start = base + i * FW + k * other
                    step = FW + other
                    v = sums[:, start:start + n * step].rearrange("p (i w) -> p w i", w=step)
                    return v[:, 0:(HALF - 1) * third + 1:third, :]

                for s in range(1, S + 1):
                    for i, j, n in ((0, s, HALF - s), (HALF - s, 0, s)):
                        last = nc.vector.tensor_tensor(
                            moved[:, half, :, (s - 1) * HALF + i:(s - 1) * HALF + i + n],
                            products(i, j, n), products(j, i, n), ALU.add)
            last.then_inc(moved_ready, 1)
            for r in range(Q):
                last = nc.vector.tensor_copy(
                    sq_cols[:, :, r * F:(r + 1) * F], left[:, r * F8:(r + 1) * F8, CROSS:FW])
            last.then_inc(squares_copied, 1)
            dve.wait_ge(squares_copied, 1)
            for r in range(Q):
                half = 1 - r * F8 // HALF
                other, third = (HALF, 1) if half == 0 else (1, HALF)
                h0 = r * F8 % HALF
                start = half * HALF * FW + h0 * third
                v = sums[:, start:start + HALF * (FW + other)].rearrange("p (i w) -> p w i", w=FW + other)
                cols = sq_cols[:, :, r * F + half * HALF:r * F + (half + 1) * HALF]
                last = nc.vector.tensor_tensor(cols, cols, v[:, 0:(F8 - 1) * third + 1:third, :], ALU.add)
            last.then_inc(sq_cols_ready, 1)

            def prepare(t):
                dve.wait_ge(gathered, (t + 1) * (16 * F))
                for half in range(2):
                    last = nc.vector.transpose(
                        fields[:, half, 0:HALF, :].rearrange("p f g -> p (f g)"),
                        rows[:, half * HALF * D:(half + 1) * HALF * D])
                last.then_inc(rows_turned, 1)
                dve.wait_ge(rows_turned, t + 1)
                nc.vector.tensor_copy(fields[:, :, HALF:WRAP, :], fields[:, :, 0:S, :]).then_inc(fields_ready, 1)
                for q in range(Q):
                    own = slice(q * D, (q + 1) * D)
                    last = nc.vector.tensor_copy(
                        diag_blocks[own, :, q, :].rearrange("p g (k f) -> p g k f", k=2),
                        fields[own, :, 0:HALF, :].rearrange("p k f g -> p g k f"))
                last.then_inc(blocks_ready, 1)
                dve.wait_ge(fields_ready, t + 1)
                for part in range(2):
                    gs = slice(part * G // 2, (part + 1) * G // 2)
                    for half in range(2):
                        flat = fields[:, half, :, :].rearrange("p f g -> p (f g)")
                        for s in range(1, S + 1):
                            last = nc.vector.tensor_tensor(
                                pairs[:, gs, half, (s - 1) * HALF:s * HALF],
                                fields[:, half, 0:HALF, gs].rearrange("p f g -> p g f"),
                                fields[:, half, s:s + HALF, gs].rearrange("p f g -> p g f"), ALU.mult)
                    last.then_inc(pairs_ready, 1)

            dve.wait_ge(blocks_cleared, 1)
            prepare(0)

            def save_quads(t):
                for k in range(NQ):
                    dve.wait_ge(quad_formed, t * NQ + k + 1)
                    nc.vector.tensor_copy(tri[0:PAIRS, 1, :, k * QUAD * Q:(k + 1) * QUAD * Q],
                                          quad_banks[1][k % 2][0:PAIRS]).then_inc(quad_saved_dve, 1)

            save_quads(0)
            with dve.Fori(1, T) as t:
                prepare(t)
                dve.wait_ge(x_summed, t)
                save_quads(t)

        @block.scalar
        def _(act):
            act.wait_ge(w0_turned, 1)
            nc.scalar.copy(w0_t.rearrange("p (r f) c -> p f r c", f=F8),
                           psum[:, 0:2, :].rearrange("p b (f r c) -> p (b f) r c", f=HPB, r=Q)
                           ).then_inc(w0_t_saved, 1)
            act.wait_ge(dense_turned, 1)
            nc.scalar.copy(dense_t[:, :, :].rearrange("p t (g q) -> p t q g", q=Q),
                           psum[0:CTX, 2, :].rearrange("p (t q g) -> p t q g", t=T, q=Q)
                           ).then_inc(dense_saved, 1)
            for k in range(F // 2):
                act.wait_ge(left_formed, k + 1)
                b = 2 + 2 * (k % 3)
                nc.scalar.copy(left[:, 2 * k:2 * k + 2, :], psum[:, b:b + 2, 0:FW]).then_inc(left_saved, 1)
            for k in range(NV):
                act.wait_ge(v_formed, k + 1)
                source = psum[:, k % 8, :]
                if k < NV - 2:
                    half, h = v_order(k)
                    nc.scalar.copy(v_pair[0:PAIRS, half, h:h + HPB, :].rearrange("p h j -> p (h j)"),
                                   source[0:PAIRS]).then_inc(v_saved, 1)
                else:
                    n = k - (NV - 2)
                    nc.scalar.copy(v_square[:, n * HPB:(n + 1) * HPB, :].rearrange("p h j -> p (h j)"),
                                   source).then_inc(v_saved, 1)

            def form_squares(t):
                act.wait_ge(fields_ready, t + 1)
                source = fields[:, :, 0:HALF, :].rearrange("p k f g -> p g k f")
                for kind, fn in ((0, ACT.Square), (1, ACT.Copy)):
                    nc.scalar.activation(squares_v[:, :, kind, :].rearrange("p g (k f) -> p g k f", k=2),
                                         source, fn).then_inc(squares_ready, 1)

            def save_quad(t, k):
                act.wait_ge(quad_formed, t * NQ + k + 1)
                columns = slice(k * QUAD * Q, (k + 1) * QUAD * Q)
                nc.scalar.copy(tri[0:PAIRS, 0, :, columns], quad_banks[0][k % 2][0:PAIRS])
                nc.scalar.copy(wide[:, :, columns], quad_banks[2][k % 2][0:2 * F]).then_inc(quad_saved_act, 1)

            def hidden(summed, dst, src, bias, done, t, m):
                act.wait_ge(summed, t + 1)
                for i in range(m):
                    last = nc.scalar.activation(dst[:, i, :], src[:, i, :], ACT.Relu, bias=bias[:, i:i + 1])
                last.then_inc(done, 1)

            def tower_step(k, t):
                if k == 1:
                    hidden(h1_summed, hid1, ps_h1, bias1, h1_ready, t, M1)
                if k == 3:
                    hidden(h2_summed, hid2, ps_h2, bias2, h2_ready, t, M2)
                if k == 5:
                    act.wait_ge(y_summed, t + 1)
                    nc.scalar.copy(y_row[:, bass.ds(t * P, P)].rearrange("p (q g) -> p g q", q=Q),
                                   ps_y.rearrange("p (g q) -> p g q", q=Q)).then_inc(y_saved, 1)

            def save_x(t):
                act.wait_ge(x_summed, t + 1)
                nc.scalar.copy(inter[:, :, :], ps_x).then_inc(x_saved, 1)

            act.wait_ge(tower_loaded, 16 * 7)
            form_squares(0)
            for k in range(NQ):
                save_quad(0, k)
            with act.Fori(1, T) as t:
                form_squares(t)
                save_x(t - 1)
                for k in range(NQ):
                    save_quad(t, k)
                    tower_step(k, t - 1)
            save_x(T - 1)
            for k in range(NQ):
                tower_step(k, T - 1)

        @block.tensor
        def _(pe):
            def mm(*args, **kw):
                return nc.tensor.matmul(*args, **kw)

            pe.wait_ge(ident_ready, 1)
            pe.wait_ge(w0_loaded, 16 * Q)
            for f in range(F8):
                last = nc.tensor.transpose(psum[:, f // HPB, f % HPB * P:(f % HPB + 1) * P],
                                           w0_sb[:, f, :], ident[:, :])
            last.then_inc(w0_turned, 1)
            pe.wait_ge(tower_loaded, 16 * 7)
            for t in range(T):
                last = nc.tensor.transpose(psum[0:CTX, 2, t * P:(t + 1) * P], dense[:, t, :], ident[:, :])
            last.then_inc(dense_turned, 1)

            pe.wait_ge(w1_loaded, 16)
            pe.wait_ge(w_cross_ready, 1)
            pe.wait_ge(dense_saved, 1)
            for k in range(F // 2):
                if k >= 3:
                    pe.wait_ge(left_saved, k - 2)
                for n in range(2):
                    last = mm(psum[:, 2 + 2 * (k % 3) + n, 0:FW], w1_sb[:, 2 * k + n, :], w_cross[:, :],
                              start=True, stop=True)
                last.then_inc(left_formed, 1)

            pe.wait_ge(w_pair_ready, 1)
            pe.wait_ge(w0_t_saved, 1)
            for k in range(NV - 2):
                half, h = v_order(k)
                own = h // HALF == half
                if k == 0:
                    pe.wait_ge(left_saved, F // 2)
                if not own:
                    pe.wait_ge(moved_ready, 1)
                if k >= 8:
                    pe.wait_ge(v_saved, k - 7)
                last = mm(psum[0:PAIRS, k % 8, :], w_pair[:, half, 0:PAIRS], w1_sb[:, h:h + HPB, :],
                          start=True, stop=own)
                if not own:
                    for n in range(HPB):
                        last = mm(psum[0:PAIRS, k % 8, n * J:(n + 1) * J],
                                  moved[:, half, h % HALF + n, 0:PAIRS], ident[:, :],
                                  start=False, stop=n == HPB - 1)
                last.then_inc(v_formed, 1)
            pe.wait_ge(sq_cols_ready, 1)
            for k in range(NV - 2, NV):
                pe.wait_ge(v_saved, k - 7)
                for n in range(HPB):
                    last = nc.tensor.transpose(psum[:, k % 8, n * J:(n + 1) * J],
                                               sq_cols[:, (k - NV + 2) * HPB + n, :], ident[:, :])
                last.then_inc(v_formed, 1)

            def form_quad(t, k, first=False):
                if k == 0:
                    pe.wait_ge(blocks_ready, t + 1)
                    pe.wait_ge(squares_ready, 2 * (t + 1))
                if k % (NQ // 2) == 0:
                    pe.wait_ge(pairs_ready, 2 * t + 1 + k // (NQ // 2))
                if not first:
                    pe.wait_ge(quad_saved_act, t * NQ + k - 1)
                    pe.wait_ge(quad_saved_dve, t * NQ + k - 1)
                for n in range(QUAD):
                    g = k * QUAD + n
                    blocks = diag_blocks[:, g, :, :].rearrange("p q h -> p (q h)")
                    for kind, lhs in enumerate((pairs[:, g, 0, 0:PAIRS], pairs[:, g, 1, 0:PAIRS],
                                                squares[:, g * 2 * F:(g + 1) * 2 * F])):
                        last = mm(psum[0:lhs.shape[1], 2 * kind + k % 2, n * P:(n + 1) * P], lhs, blocks,
                                  start=True, stop=True)
                last.then_inc(quad_formed, 1)

            def contract(t):
                pe.wait_ge(quad_saved_act, (t + 1) * NQ)
                pe.wait_ge(quad_saved_dve, (t + 1) * NQ)
                for half in range(2):
                    for h in range(F):
                        mm(ps_x[:, 1, :], v_pair[0:PAIRS, half, h, :], tri[0:PAIRS, half, h, :],
                           start=half == 0 and h == 0, stop=False)
                pe.wait_ge(wide_packed, (t + 1) * PACKS)
                for f in range(F8):
                    mm(ps_x[:, 1, :], v_square[:, f, :], packed[:, 0, f, :], start=False, stop=f == F8 - 1)
                for f in range(F8):
                    last = mm(ps_x[:, 0, :], w0_sb[:, f, :], packed[:, 1, f, :], start=f == 0, stop=f == F8 - 1)
                last.then_inc(x_summed, 1)

            def tower_step(k, t):
                if k == 1:
                    pe.wait_ge(x_saved, t + 1)
                    for m in range(M1):
                        cols = slice(m * P, (m + 1) * P)
                        mm(ps_h1[:, m, :], top1[:, 0, cols], inter[:, 0, :], start=True, stop=False)
                        mm(ps_h1[:, m, :], top1[:, 1, cols], inter[:, 1, :], start=False, stop=False)
                        last = mm(ps_h1[:, m, :], top1_ctx[:, cols], dense_t[:, bass.ds(t, 1), :],
                                  start=False, stop=True)
                    last.then_inc(h1_summed, 1)
                if k == 3:
                    pe.wait_ge(h1_ready, t + 1)
                    for m in range(M2):
                        for i in range(M1):
                            last = mm(ps_h2[:, m, :], top2[:, i, m * P:(m + 1) * P], hid1[:, i, :],
                                      start=i == 0, stop=i == M1 - 1)
                    last.then_inc(h2_summed, 1)
                if k == 5:
                    pe.wait_ge(h2_ready, t + 1)
                    for i in range(M2):
                        last = mm(ps_y, top3[:, i:i + 1], hid2[:, i, :], start=i == 0, stop=i == M2 - 1)
                    last.then_inc(y_summed, 1)

            pe.wait_ge(v_saved, NV)
            for k in range(NQ):
                form_quad(0, k, first=k < 2)
            contract(0)
            with pe.Fori(1, T) as t:
                for k in range(NQ):
                    form_quad(t, k)
                    tower_step(k, t - 1)
                contract(t)
            for k in range(NQ):
                tower_step(k, T - 1)


def kernel(**inputs):
    import numpy as np
    import concourse.bacc as bacc
    from concourse.bass_utils import run_bass_kernel_spmd

    nc = bacc.Bacc("TRN2", target_bir_lowering=False, num_devices=1)
    arrays = {}

    def dram(name):
        a = np.ascontiguousarray(inputs[name])
        arrays["in_" + name] = a
        return nc.dram_tensor("in_" + name, a.shape, mybir.dt.from_np(a.dtype), kind="ExternalInput").ap()

    tables = [dram(f"tbl_{f}") for f in range(F)]
    args = {name: dram(name) for name in ("dense_ctx", "ids", "W_top1", "b_top1", "W_top2", "b_top2", "W_top3",
                                          "L0_rec_W0", "L0_rec_W1")}
    out = nc.dram_tensor("out", (B, 1), FP32, kind="ExternalOutput").ap()
    build(nc, args["dense_ctx"], args["ids"], tables, args["W_top1"], args["b_top1"], args["W_top2"],
          args["b_top2"], args["W_top3"], args["L0_rec_W0"], args["L0_rec_W1"], out)
    result = run_bass_kernel_spmd(nc, [arrays], core_ids=[0])
    return result.results[0]["out"]
```

```python
from contextlib import ExitStack

import concourse.bass as bass
from concourse import mybir

FP32 = mybir.dt.float32
INT32 = mybir.dt.int32
ALU = mybir.AluOpType
ACT = mybir.ActivationFunctionType

P = 128
B, F, D = 512, 32, 32
J = 128
CTX = 16
N1, N2 = 512, 256
T = B // P
Q = P // D
G = P // Q
HALF = F // 2
F4 = F // 4
NEXT = F4 // 2
WRAP = F4 + NEXT
NEAR = 4 * F4 * (F4 - 1) // 2
SQ = F4 * F4
FAR = 2 * SQ
PAIRS = NEAR + FAR
CROSS = HALF * HALF
LW = SQ + CROSS + F
BANK = 512
QUAD = BANK // P
NQ = G // QUAD
HPB = BANK // J
M1, M2 = N1 // P, N2 // P


def build(nc, dense_ctx, ids, tables, w_top1, b_top1, w_top2, b_top2, w_top3, w0, w1, out):
    with ExitStack() as ctx:
        def sbuf(name, shape, dt=FP32):
            return ctx.enter_context(nc.sbuf_tensor(name, shape, dt))

        def sem(name):
            return ctx.enter_context(nc.semaphore(name))

        idx = sbuf("idx", [P, T, F], INT32)
        rows = sbuf("rows", [P, F * D])
        fields = sbuf("fields", [P, 4, WRAP, G])
        diag_blocks = sbuf("diag_blocks", [P, G, Q, F])
        pairs = sbuf("pairs", [P, G, PAIRS])
        squares = sbuf("squares", [P, G * 2 * F])
        squares_v = squares[:, :].rearrange("p (g k f) -> p g k f", g=G, k=2)
        sums = sbuf("sums", [P, (F + HALF + 2 * F4 + F) * P])
        at = F * P
        near = sums[0:NEAR, 0:at].rearrange("p (h x) -> p h x", h=F)
        far = sums[:, at:at + HALF * P].rearrange("p (h x) -> p h x", h=HALF)
        at += HALF * P
        packed = sums[:, at:at + 2 * F4 * P].rearrange("p (k f x) -> p k f x", k=2, f=F4)
        at += 2 * F4 * P
        wide = sums[0:2 * F, at:at + F * P].rearrange("p (h x) -> p h x", h=F)
        w1_sb = sbuf("w1_sb", [P, F, J])
        w0_sb = sbuf("w0_sb", [P, F4, J])
        w0_t = squares[:, 0:F * F].rearrange("p (a c) -> p a c", a=F)
        w0_wrap = squares[:, F * F:F * F + F * WRAP].rearrange("p (u a c) -> p u a c", u=4, a=F4)
        w_near = sbuf("w_near", [P, NEAR])
        w_rest = sbuf("w_rest", [P, FAR + CROSS + F])
        v_near = sbuf("v_near", [P, F, J])
        v_far = sbuf("v_far", [P, HALF, J])
        v_square = sbuf("v_square", [P, F4, J])
        moved_near = sbuf("moved_near", [P, F, NEAR])
        late = sbuf("late", [P, F4 * P])
        moved_far = [part.rearrange("p (h r) -> p h r", h=F4)
                     for part in (sums[:, F * LW:F * LW + F4 * P], late[:, :])]
        moved_square = squares[:, 0:F4 * P].rearrange("p (f r) -> p f r", f=F4)
        ident = sbuf("ident", [P, P])
        top1 = sbuf("top1", [P, 2, N1])
        top1_ctx = sbuf("top1_ctx", [CTX, N1])
        top2 = sbuf("top2", [P, M1, N2])
        top3 = sbuf("top3", [P, M2])
        bias1 = sbuf("bias1", [P, M1])
        bias2 = sbuf("bias2", [P, M2])
        dense = sbuf("dense", [P, T, CTX])
        dense_t = sbuf("dense_t", [CTX, T, P])
        inter = late[:, 0:2 * P].rearrange("p (k x) -> p k x", k=2)
        hid1 = late[:, 2 * P:(2 + M1) * P].rearrange("p (m x) -> p m x", m=M1)
        hid2 = late[:, (2 + M1) * P:(2 + M1 + M2) * P].rearrange("p (m x) -> p m x", m=M2)
        y_row = sbuf("y_row", [1, B])

        psum = ctx.enter_context(nc.psum_tensor("psum", [P, 8, BANK], FP32))
        quad_banks = [[psum[:, 2 * kind + n, :].rearrange("p (x h) -> p h x", h=F) for n in range(2)]
                      for kind in range(3)]
        ps_x = psum[:, 6, 0:2 * P].rearrange("p (k x) -> p k x", k=2)
        ps_h1 = psum[:, 7, :].rearrange("p (m x) -> p m x", m=M1)
        ps_h2 = psum[:, 7, 0:M2 * P].rearrange("p (m x) -> p m x", m=M2)
        ps_y = psum[0:1, 7, M2 * P:(M2 + 1) * P]

        def view(flat, start, *dims):
            return bass.AP(flat.tensor, flat.offset + start, [flat.ap[0], *dims])

        def left_at(h, a, c):
            a, c = min(a, c), max(a, c)
            second = h >= HALF
            if a < HALF <= c:
                at = SQ + a * HALF + c - HALF
            elif c < HALF:
                at = a * F4 + c - F4
            else:
                at = SQ + CROSS + F + (a - HALF) * F4 + c - HALF - F4
            return h * LW + at - second * SQ

        def squares_at(h):
            return h * LW + SQ + CROSS - (h >= HALF) * SQ

        def others(quarter):
            half = quarter // 2
            return ((4 * half + 1 - quarter) * F4, F4), ((1 - half) * HALF, HALF)

        def near_row(s, quarter, i):
            return (s - 1) * F + quarter * (F4 if s < NEXT else F4 // 2) + i

        ids_loaded = sem("ids_loaded")
        w0_loaded = sem("w0_loaded")
        w1_loaded = [sem(f"w1_loaded{n}") for n in range(4)]
        tower_loaded = sem("tower_loaded")
        ident_cleared = sem("ident_cleared")
        ident_ready = sem("ident_ready")
        blocks_cleared = sem("blocks_cleared")
        gathered = sem("gathered")
        rows_turned = sem("rows_turned")
        fields_ready = sem("fields_ready")
        products_ready = sem("products_ready")
        squares_ready = sem("squares_ready")
        w0_turned = sem("w0_turned")
        w0_t_saved = sem("w0_t_saved")
        dense_turned = sem("dense_turned")
        dense_saved = sem("dense_saved")
        w_rest_ready = sem("w_rest_ready")
        w0_wrapped = sem("w0_wrapped")
        w_near_ready = sem("w_near_ready")
        near_cleared = sem("near_cleared")
        left_formed = sem("left_formed")
        left_saved = sem("left_saved")
        moved_far_ready = sem("moved_far_ready")
        moved_near_ready = sem("moved_near_ready")
        squares_copied = sem("squares_copied")
        moved_square_ready = sem("moved_square_ready")
        v_formed = sem("v_formed")
        v_saved = sem("v_saved")
        v_turned = sem("v_turned")
        v_added = sem("v_added")
        v_square_turned = sem("v_square_turned")
        v_square_saved = sem("v_square_saved")
        quad_formed = sem("quad_formed")
        quad_saved_act = sem("quad_saved_act")
        quad_saved_dve = sem("quad_saved_dve")
        wide_packed = sem("wide_packed")
        x_summed = sem("x_summed")
        x_saved = sem("x_saved")
        h1_summed = sem("h1_summed")
        h1_ready = sem("h1_ready")
        h2_summed = sem("h2_summed")
        h2_ready = sem("h2_ready")
        y_summed = sem("y_summed")
        y_saved = sem("y_saved")
        y_stored = sem("y_stored")
        block = ctx.enter_context(nc.Block())

        NF, NN = HALF // HPB, F // HPB
        PACKS = 16 * 2 * Q
        w0_v = w0.rearrange("(r f c) j -> r c f j", r=Q, f=F4)

        @block.sync
        def _(sp):
            sp.dma_start(idx[:, :, :], ids.rearrange("(t p) f -> p t f", p=P)).then_inc(ids_loaded, 16)
            for r in (0, 1):
                sp.dma_start(w0_sb[r * F:(r + 1) * F, :, :], w0_v[r]).then_inc(w0_loaded, 16)
            w1_v = w1.rearrange("(h m) j -> m h j", m=J)
            for n in range(4):
                part = slice(n * F4, (n + 1) * F4)
                sp.dma_start(w1_sb[:, part, :], w1_v[:, part, :]).then_inc(w1_loaded[n], 16)
            with nc.allow_non_contiguous_dma(reason="a few hundred biases"):
                for dst, src in (
                    (dense[:, :, :], dense_ctx.rearrange("(t p) c -> p t c", p=P)),
                    (top1[:, :, :], w_top1[0:2 * J, :].rearrange("(k p) n -> p k n", p=P)),
                    (top1_ctx[:, :], w_top1[2 * J:2 * J + CTX, :]),
                    (top2[:, :, :], w_top2.rearrange("(k p) n -> p k n", p=P)),
                    (top3[:, :], w_top3.rearrange("(k p) n -> p (k n)", p=P)),
                    (bias1[:, :], b_top1.rearrange("(k p) -> p k", p=P)),
                    (bias2[:, :], b_top2.rearrange("(k p) -> p k", p=P)),
                ):
                    sp.dma_start(dst, src).then_inc(tower_loaded, 16)

            with sp.Fori(0, T) as t:
                sp.wait_ge(quad_saved_act, t * NQ + NQ)
                for kind in range(2):
                    for r in range(Q):
                        sp.dma_start(packed[r * F:(r + 1) * F, kind, :, :],
                                     wide[kind * F:(kind + 1) * F, r * F4:(r + 1) * F4, :]
                                     ).then_inc(wide_packed, 16)
            sp.wait_ge(y_saved, T)
            sp.dma_start(out.rearrange("b o -> o b"), y_row[:, :]).then_inc(y_stored, 16)
            sp.wait_ge(y_stored, 16)

        @block.gpsimd
        def _(pool):
            nc.gpsimd.memset(ident[:, :], 0.0).then_inc(ident_cleared, 1)
            pool.wait_ge(ident_cleared, 1)
            nc.gpsimd.affine_select(out=ident[:, :], in_=ident[:, :], compare_op=ALU.not_equal, fill=1.0,
                                    base=0, pattern=[[-1, P]], channel_multiplier=1).then_inc(ident_ready, 1)
            pool.wait_ge(ids_loaded, 16)
            for t in range(T):
                if t:
                    pool.wait_ge(rows_turned, t)
                for f in range(F):
                    pool.indirect_dma_start(rows[:, f * D:(f + 1) * D], None, tables[f],
                                            bass.IndirectOffsetOnAxis(idx[:, t, f:f + 1], 0)
                                            ).then_inc(gathered, 16)

        @block.vector
        def _(dve):
            nc.vector.memset(diag_blocks[:, :, :, :], 0.0).then_inc(blocks_cleared, 1)

            nc.vector.memset(moved_near[:, :, :], 0.0).then_inc(near_cleared, 1)

            dve.wait_ge(w0_t_saved, 1)
            swapped = w0_t.rearrange("p a c -> p c a")
            for at, first, second in ((0, (0, F4), (F4, HALF)), (SQ, (0, HALF), (HALF, F)),
                                      (SQ + CROSS + F, (HALF, HALF + F4), (HALF + F4, F))):
                a, c = slice(*first), slice(*second)
                n = (a.stop - a.start) * (c.stop - c.start)
                nc.vector.tensor_tensor(w_rest[:, at:at + n].rearrange("p (a c) -> p a c", a=a.stop - a.start),
                                        w0_t[:, a, c], swapped[:, a, c], ALU.add)
            nc.vector.tensor_copy(w_rest[:, SQ + CROSS:SQ + CROSS + F], squares[:, 0:F * F:F + 1]
                                  ).then_inc(w_rest_ready, 1)
            quarter_step = (F4 * (F + 1), 4)
            for at, n in ((0, F4), (F4, NEXT)):
                last = nc.vector.tensor_tensor(
                    w0_wrap[:, :, :, at:at + n], view(squares[:, :], 0, quarter_step, (F, F4), (1, n)),
                    view(squares[:, :], 0, quarter_step, (1, F4), (F, n)), ALU.add)
            last.then_inc(w0_wrapped, 1)
            dve.wait_ge(w0_wrapped, 1)
            for s in range(1, NEXT + 1):
                n = F4 if s < NEXT else F4 // 2
                start = near_row(s, 0, 0)
                last = nc.vector.tensor_copy(
                    w_near[:, start:start + 4 * n].rearrange("p (u i) -> p u i", u=4),
                    view(squares[:, :], F * F + s, (F4 * WRAP, 4), (WRAP + 1, n)))
            last.then_inc(w_near_ready, 1)

            left = sums[:, 0:F * LW]

            def left_view(h, a, c, steps):
                here = left_at(h, a, c)
                return view(left, here, *((left_at(h + x, a + y, c + z) - here, n) for (x, y, z), n in steps))

            dve.wait_ge(near_cleared, 1)
            for half in range(2):
                dve.wait_ge(left_saved, (half + 1) * F // 4)
                i, j, c = half * HALF, half * HALF + F4, (1 - half) * HALF
                for n in range(2):
                    dst = moved_far[n][:, :, half * SQ:(half + 1) * SQ].rearrange("p h (i j) -> p h i j", i=F4)
                    last = nc.vector.tensor_tensor(
                        dst,
                        left_view(i, j, c + n * F4, (((0, 0, 1), F4), ((1, 0, 0), F4), ((0, 1, 0), F4))),
                        left_view(j, i, c + n * F4, (((0, 0, 1), F4), ((0, 1, 0), F4), ((1, 0, 0), F4))), ALU.add)
                last.then_inc(moved_far_ready, 1)
                for quarter in (2 * half, 2 * half + 1):
                    for s in range(1, NEXT + 1):
                        runs = ((0, s, F4 - s), (F4 - s, 0, s)) if s < NEXT else ((0, s, s),)
                        for i, j, n in runs:
                            row = near_row(s, quarter, i)
                            i, j = i + quarter * F4, j + quarter * F4
                            for c, nc_ in others(quarter):
                                last = nc.vector.tensor_tensor(
                                    moved_near[:, c:c + nc_, row:row + n],
                                    left_view(i, j, c, (((0, 0, 1), nc_), ((1, 1, 0), n) if n > 1 else ((0, 0, 0), 1))),
                                    left_view(j, i, c, (((0, 0, 1), nc_), ((1, 1, 0), n) if n > 1 else ((0, 0, 0), 1))),
                                    ALU.add)
                last.then_inc(moved_near_ready, 1)
            for r in range(Q):
                last = nc.vector.tensor_copy(moved_square[:, :, r * F:(r + 1) * F],
                                             view(left, squares_at(r * F4), (LW, F4), (1, F)))
            last.then_inc(squares_copied, 1)
            dve.wait_ge(squares_copied, 1)
            for r in range(Q):
                for i, n in others(r):
                    cols = moved_square[:, :, r * F + i:r * F + i + n]
                    last = nc.vector.tensor_tensor(
                        cols, cols, left_view(i, i, r * F4, (((0, 0, 1), F4), ((1, 1, 0), n))), ALU.add)
            last.then_inc(moved_square_ready, 1)

            def add_moved(k):
                dve.wait_ge(v_saved, k + 1)
                dve.wait_ge(v_turned, k + 1)
                if k < NF:
                    v, turned = v_far[:, k * HPB:(k + 1) * HPB, :], psum[:, NF + k, :]
                else:
                    n = k - NF
                    v, turned = v_near[0:NEAR, n * HPB:(n + 1) * HPB, :], psum[0:NEAR, 6 + n % 2, :]
                v = v.rearrange("p h j -> p (h j)")
                nc.vector.tensor_tensor(v, v, turned, ALU.add).then_inc(v_added, 1)

            def prepare(t):
                dve.wait_ge(gathered, (t + 1) * (16 * F))
                for u in range(4):
                    last = nc.vector.transpose(fields[:, u, 0:F4, :].rearrange("p f g -> p (f g)"),
                                               rows[:, u * F4 * D:(u + 1) * F4 * D])
                last.then_inc(rows_turned, 1)
                dve.wait_ge(rows_turned, t + 1)
                nc.vector.tensor_copy(fields[:, :, F4:WRAP, :], fields[:, :, 0:NEXT, :]).then_inc(fields_ready, 1)
                dve.wait_ge(fields_ready, t + 1)
                for part in range(2):
                    gs = slice(part * G // 2, (part + 1) * G // 2)
                    for q in range(Q):
                        own = slice(q * D, (q + 1) * D)
                        nc.vector.tensor_copy(
                            diag_blocks[own, gs, q, :].rearrange("p g (u f) -> p g u f", u=4),
                            fields[own, :, 0:F4, gs].rearrange("p u f g -> p g u f"))
                    by_group = fields[:, :, :, gs].rearrange("p u f g -> p g u f")
                    for s in range(1, NEXT + 1):
                        n = F4 if s < NEXT else F4 // 2
                        start = near_row(s, 0, 0)
                        nc.vector.tensor_tensor(
                            pairs[:, gs, start:start + 4 * n].rearrange("p g (u i) -> p g u i", u=4),
                            by_group[:, :, :, 0:n], by_group[:, :, :, s:s + n], ALU.mult)
                    for half in range(2):
                        start = NEAR + half * SQ
                        shape = [P, G // 2, F4, F4]
                        last = nc.vector.tensor_tensor(
                            pairs[:, gs, start:start + SQ].rearrange("p g (i j) -> p g i j", i=F4),
                            by_group[:, :, 2 * half, 0:F4].unsqueeze(3).to_broadcast(shape),
                            by_group[:, :, 2 * half + 1, 0:F4].unsqueeze(2).to_broadcast(shape), ALU.mult)
                    last.then_inc(products_ready, 1)

            def save_quad(t, k):
                dve.wait_ge(quad_formed, t * NQ + k + 1)
                for half in range(2):
                    own = slice(half * SQ, (half + 1) * SQ)
                    last = nc.vector.tensor_copy(
                        far[own, :, k * QUAD * Q:(k + 1) * QUAD * Q],
                        quad_banks[1][k % 2][own, (1 - half) * HALF:(2 - half) * HALF, :])
                last.then_inc(quad_saved_dve, 1)

            for k in range(NF):
                add_moved(k)
            dve.wait_ge(blocks_cleared, 1)
            prepare(0)
            for n in range(2):
                add_moved(NF + n)
            for k in range(NQ):
                save_quad(0, k)
                if k < NN - 2:
                    add_moved(NF + 2 + k)
            with dve.Fori(1, T) as t:
                prepare(t)
                dve.wait_ge(x_summed, t)
                for k in range(NQ):
                    save_quad(t, k)

        @block.scalar
        def _(act):
            for r in (2, 3):
                act.dma_start(w0_sb[r * F:(r + 1) * F, :, :], w0_v[r]).then_inc(w0_loaded, 16)
            act.wait_ge(w0_turned, 1)
            nc.scalar.copy(w0_t.rearrange("p (r f) c -> p f r c", f=F4),
                           psum[:, 0:2, :].rearrange("p b (f r c) -> p (b f) r c", f=HPB, r=Q)
                           ).then_inc(w0_t_saved, 1)
            for k in range(F // 2):
                act.wait_ge(left_formed, k + 1)
                b = 2 + 2 * (k % 3)
                nc.scalar.copy(sums[:, 2 * k * LW:2 * (k + 1) * LW].rearrange("p (h w) -> p h w", h=2),
                               psum[:, b:b + 2, 0:LW]).then_inc(left_saved, 1)
            for k in range(NF + NN):
                act.wait_ge(v_formed, k + 1)
                v = v_far[:, k * HPB:(k + 1) * HPB, :] if k < NF else \
                    v_near[0:NEAR, (k - NF) * HPB:(k - NF + 1) * HPB, :]
                nc.scalar.copy(v.rearrange("p h j -> p (h j)"), psum[0:v.shape[0], k % 4, :]).then_inc(v_saved, 1)
            act.wait_ge(v_square_turned, 1)
            nc.scalar.copy(v_square[:, :, :].rearrange("p h j -> p (h j)"),
                           psum[:, 4:6, :].rearrange("p b n -> p (b n)")).then_inc(v_square_saved, 1)
            act.wait_ge(dense_turned, 1)
            nc.scalar.copy(dense_t[:, :, :].rearrange("p t (g q) -> p t q g", q=Q),
                           psum[0:CTX, 0, :].rearrange("p (t q g) -> p t q g", t=T, q=Q)
                           ).then_inc(dense_saved, 1)

            def form_squares(t):
                act.wait_ge(fields_ready, t + 1)
                source = fields[:, :, 0:F4, :].rearrange("p u f g -> p g u f")
                for kind, fn in ((0, ACT.Square), (1, ACT.Copy)):
                    nc.scalar.activation(squares_v[:, :, kind, :].rearrange("p g (u f) -> p g u f", u=4),
                                         source, fn).then_inc(squares_ready, 1)

            def save_quad(t, k):
                act.wait_ge(quad_formed, t * NQ + k + 1)
                columns = slice(k * QUAD * Q, (k + 1) * QUAD * Q)
                nc.scalar.copy(near[:, :, columns], quad_banks[0][k % 2][0:NEAR])
                nc.scalar.copy(wide[:, :, columns], quad_banks[2][k % 2][0:2 * F]).then_inc(quad_saved_act, 1)

            def hidden(summed, dst, src, bias, done, t, m):
                act.wait_ge(summed, t + 1)
                for i in range(m):
                    last = nc.scalar.activation(dst[:, i, :], src[:, i, :], ACT.Relu, bias=bias[:, i:i + 1])
                last.then_inc(done, 1)

            def tower_step(k, t):
                if k == 0:
                    hidden(h1_summed, hid1, ps_h1, bias1, h1_ready, t, M1)
                if k == 1:
                    hidden(h2_summed, hid2, ps_h2, bias2, h2_ready, t, M2)
                if k == 2:
                    act.wait_ge(y_summed, t + 1)
                    nc.scalar.copy(y_row[:, bass.ds(t * P, P)].rearrange("p (q g) -> p g q", q=Q),
                                   ps_y.rearrange("p (g q) -> p g q", q=Q)).then_inc(y_saved, 1)

            def save_x(t):
                act.wait_ge(x_summed, t + 1)
                nc.scalar.copy(inter[:, :, :], ps_x).then_inc(x_saved, 1)

            act.wait_ge(tower_loaded, 16 * 7)
            form_squares(0)
            for k in range(NQ):
                save_quad(0, k)
            with act.Fori(1, T) as t:
                form_squares(t)
                save_x(t - 1)
                for k in range(NQ):
                    save_quad(t, k)
                    if k == 5:
                        tower_step(0, t - 1)
                tower_step(1, t - 1)
                tower_step(2, t - 1)
            save_x(T - 1)
            for k in range(3):
                tower_step(k, T - 1)

        @block.tensor
        def _(pe):
            def mm(*args, **kw):
                return nc.tensor.matmul(*args, **kw)

            pe.wait_ge(ident_ready, 1)
            pe.wait_ge(w0_loaded, 16 * Q)
            for f in range(F4):
                last = nc.tensor.transpose(psum[:, f // HPB, f % HPB * P:(f % HPB + 1) * P],
                                           w0_sb[:, f, :], ident[:, :])
            last.then_inc(w0_turned, 1)

            pe.wait_ge(w_rest_ready, 1)
            for k in range(F // 2):
                if 2 * k % F4 == 0:
                    pe.wait_ge(w1_loaded[2 * k // F4], 16)
                if k >= 3:
                    pe.wait_ge(left_saved, k - 2)
                start = 0 if 2 * k < HALF else SQ
                for n in range(2):
                    last = mm(psum[:, 2 + 2 * (k % 3) + n, 0:LW], w1_sb[:, 2 * k + n, :],
                              w_rest[:, start:start + LW], start=True, stop=True)
                last.then_inc(left_formed, 1)

            pe.wait_ge(left_saved, F // 2)
            for k in range(NF):
                for half in range(2):
                    at, h = half * (SQ + CROSS + F), (1 - half) * HALF + k * HPB
                    last = mm(psum[half * SQ:(half + 1) * SQ, k, :], w_rest[:, at:at + SQ],
                              w1_sb[:, h:h + HPB, :], start=True, stop=True)
                last.then_inc(v_formed, 1)
            pe.wait_ge(moved_far_ready, 2)
            for h in range(HALF):
                last = nc.tensor.transpose(psum[:, NF + h // HPB, h % HPB * J:(h % HPB + 1) * J],
                                           moved_far[h // F4][:, h % F4, :], ident[:, :])
                if h % HPB == HPB - 1:
                    last.then_inc(v_turned, 1)
            pe.wait_ge(w_near_ready, 1)
            for k in range(NN):
                pe.wait_ge(v_saved, NF + k - 3)
                mm(psum[0:NEAR, k % 4, :], w_near[:, :], w1_sb[:, k * HPB:(k + 1) * HPB, :],
                   start=True, stop=True).then_inc(v_formed, 1)
            pe.wait_ge(v_added, NF)
            pe.wait_ge(moved_square_ready, 1)
            for f in range(F4):
                last = nc.tensor.transpose(psum[:, 4 + f // HPB, f % HPB * J:(f % HPB + 1) * J],
                                           moved_square[:, f, :], ident[:, :])
            last.then_inc(v_square_turned, 1)

            def turn_near(k):
                if k >= 2:
                    pe.wait_ge(v_added, NF + k - 1)
                for n in range(HPB):
                    last = nc.tensor.transpose(psum[0:NEAR, 6 + k % 2, n * J:(n + 1) * J],
                                               moved_near[:, k * HPB + n, :], ident[:, :])
                last.then_inc(v_turned, 1)

            pe.wait_ge(moved_near_ready, 2)
            for k in range(2):
                turn_near(k)
            pe.wait_ge(tower_loaded, 16 * 7)
            pe.wait_ge(v_saved, NF + NN)
            for t in range(T):
                last = nc.tensor.transpose(psum[0:CTX, 0, t * P:(t + 1) * P], dense[:, t, :], ident[:, :])
            last.then_inc(dense_turned, 1)

            def form_quad(t, k, first=False):
                if k == 0:
                    pe.wait_ge(squares_ready, 2 * (t + 1))
                if k % (NQ // 2) == 0:
                    pe.wait_ge(products_ready, 2 * t + 1 + k // (NQ // 2))
                if not first:
                    pe.wait_ge(quad_saved_act, t * NQ + k - 1)
                    pe.wait_ge(quad_saved_dve, t * NQ + k - 1)
                for n in range(QUAD):
                    g = k * QUAD + n
                    blocks = diag_blocks[:, g, :, :].rearrange("p q h -> p (q h)")
                    for kind, lhs in enumerate((pairs[:, g, 0:NEAR], pairs[:, g, NEAR:PAIRS],
                                                squares[:, g * 2 * F:(g + 1) * 2 * F])):
                        last = mm(psum[0:lhs.shape[1], 2 * kind + k % 2, n * P:(n + 1) * P], lhs, blocks,
                                  start=True, stop=True)
                last.then_inc(quad_formed, 1)

            def contract(t, behind=None):
                pe.wait_ge(quad_saved_act, (t + 1) * NQ)
                pe.wait_ge(quad_saved_dve, (t + 1) * NQ)
                for h in range(F):
                    mm(ps_x[:, 1, :], v_near[0:NEAR, h, :], near[:, h, :], start=h == 0, stop=False)
                if behind is not None:
                    behind()
                for h in range(HALF):
                    mm(ps_x[:, 1, :], v_far[:, h, :], far[:, h, :], start=False, stop=False)
                pe.wait_ge(wide_packed, (t + 1) * PACKS)
                for f in range(F4):
                    mm(ps_x[:, 1, :], v_square[:, f, :], packed[:, 0, f, :], start=False, stop=f == F4 - 1)
                for f in range(F4):
                    last = mm(ps_x[:, 0, :], w0_sb[:, f, :], packed[:, 1, f, :], start=f == 0, stop=f == F4 - 1)
                last.then_inc(x_summed, 1)

            def tower_step(k, t):
                if k == 0:
                    pe.wait_ge(x_saved, t + 1)
                    for m in range(M1):
                        cols = slice(m * P, (m + 1) * P)
                        mm(ps_h1[:, m, :], top1[:, 0, cols], inter[:, 0, :], start=True, stop=False)
                        mm(ps_h1[:, m, :], top1[:, 1, cols], inter[:, 1, :], start=False, stop=False)
                        last = mm(ps_h1[:, m, :], top1_ctx[:, cols], dense_t[:, bass.ds(t, 1), :],
                                  start=False, stop=True)
                    last.then_inc(h1_summed, 1)
                if k == 1:
                    pe.wait_ge(h1_ready, t + 1)
                    for m in range(M2):
                        for i in range(M1):
                            last = mm(ps_h2[:, m, :], top2[:, i, m * P:(m + 1) * P], hid1[:, i, :],
                                      start=i == 0, stop=i == M1 - 1)
                    last.then_inc(h2_summed, 1)
                if k == 2:
                    pe.wait_ge(h2_ready, t + 1)
                    for i in range(M2):
                        last = mm(ps_y, top3[:, i:i + 1], hid2[:, i, :], start=i == 0, stop=i == M2 - 1)
                    last.then_inc(y_summed, 1)

            for k in range(NQ):
                if k == 0:
                    pe.wait_ge(v_square_saved, 1)
                    pe.wait_ge(dense_saved, 1)
                form_quad(0, k, first=k < 2)
                if k < NN - 2:
                    turn_near(2 + k)
            pe.wait_ge(v_added, NF + NN)
            contract(0)
            with pe.Fori(1, T) as t:
                for k in range(NQ):
                    form_quad(t, k)
                    if k == 4:
                        tower_step(0, t - 1)
                tower_step(1, t - 1)
                contract(t, lambda: tower_step(2, t - 1))
            for k in range(3):
                tower_step(k, T - 1)


def kernel(**inputs):
    import numpy as np
    import concourse.bacc as bacc
    from concourse.bass_utils import run_bass_kernel_spmd

    nc = bacc.Bacc("TRN2", target_bir_lowering=False, num_devices=1)
    arrays = {}

    def dram(name):
        a = np.ascontiguousarray(inputs[name])
        arrays["in_" + name] = a
        return nc.dram_tensor("in_" + name, a.shape, mybir.dt.from_np(a.dtype), kind="ExternalInput").ap()

    tables = [dram(f"tbl_{f}") for f in range(F)]
    args = {name: dram(name) for name in ("dense_ctx", "ids", "W_top1", "b_top1", "W_top2", "b_top2", "W_top3",
                                          "L0_rec_W0", "L0_rec_W1")}
    out = nc.dram_tensor("out", (B, 1), FP32, kind="ExternalOutput").ap()
    build(nc, args["dense_ctx"], args["ids"], tables, args["W_top1"], args["b_top1"], args["W_top2"],
          args["b_top2"], args["W_top3"], args["L0_rec_W0"], args["L0_rec_W1"], out)
    result = run_bass_kernel_spmd(nc, [arrays], core_ids=[0])
    return result.results[0]["out"]
```

```python
from contextlib import ExitStack

import concourse.bass as bass
from concourse import mybir

FP32 = mybir.dt.float32
INT32 = mybir.dt.int32
ALU = mybir.AluOpType
ACT = mybir.ActivationFunctionType

P = 128
B, F, D = 512, 32, 32
J = 128
CTX = 16
N1, N2 = 512, 256
T = B // P
Q = P // D
G = P // Q
HALF = F // 2
F4 = F // 4
NEXT = F4 // 2
WRAP = F4 + NEXT
NEAR_PAIRS = 2 * F4 * (F4 - 1)
NEAR = NEAR_PAIRS + HALF
SQ = F4 * F4
FAR = 2 * SQ
PAIRS = NEAR + FAR
CROSS = HALF * HALF
LW = SQ + CROSS + HALF + SQ
WIDE = F + HALF
BANK = 512
QUAD = BANK // P
NQ = G // QUAD
SIDE = P // 2
QS = QUAD * Q // 2
PARTS = 0, 1, 2, 4, 6
NP = len(PARTS)
LEAD = 3
HPB = BANK // J
SQUARED = HALF * F // P
PACKED = F4 + SQUARED
M1, M2 = N1 // P, N2 // P


def build(nc, dense_ctx, ids, tables, w_top1, b_top1, w_top2, b_top2, w_top3, w0, w1, out):
    with ExitStack() as ctx:
        def sbuf(name, shape, dt=FP32):
            return ctx.enter_context(nc.sbuf_tensor(name, shape, dt))

        def sem(name):
            return ctx.enter_context(nc.semaphore(name))

        idx = sbuf("idx", [P, T, F], INT32)
        rows = sbuf("rows", [P, F * D])
        fields = sbuf("fields", [P, 4, WRAP, G])
        diag_blocks = sbuf("diag_blocks", [P, G, Q, F])
        pairs = sbuf("pairs", [P, G, PAIRS])
        squares = sbuf("squares", [P, G * WIDE])
        squares_v = squares[:, :].rearrange("p (g r) -> p g r", g=G)
        sums = sbuf("sums", [P, F * LW + F4 * P])
        at = F * P
        near = sums[:, 0:at].rearrange("p (h x) -> p h x", h=F)
        far = sums[:, at:at + HALF * P].rearrange("p (h x) -> p h x", h=HALF)
        at += HALF * P
        packed = sums[:, at:at + PACKED * P].rearrange("p (f x) -> p f x", f=PACKED)
        at += PACKED * P
        wide = sums[:, at:at + F * SIDE].rearrange("p (h x) -> p h x", h=F)
        w1_sb = sbuf("w1_sb", [P, F, J])
        w0_sb = sbuf("w0_sb", [P, F4, J])
        w0_rows = pairs[:, 0:5, :].rearrange("p g n -> p (g n)")[:, 0:F * F * J // P].rearrange(
            "p (k j) -> p k j", j=J)
        w0_t = squares[:, 0:F * F].rearrange("p (a c) -> p a c", a=F)
        w0_wrap = squares[:, F * F:F * F + F * WRAP].rearrange("p (u a c) -> p u a c", u=4, a=F4)
        w_near = sbuf("w_near", [P, NEAR])
        w_rest = sbuf("w_rest", [P, LW])
        v_near = sbuf("v_near", [P, F, J])
        v_far = sbuf("v_far", [P, HALF, J])
        v_square = sbuf("v_square", [P, SQUARED, J])
        moved_near = sbuf("moved_near", [P, F, NEAR])
        late = sbuf("late", [P, F4 * P])
        moved_far = [part.rearrange("p (h r) -> p h r", h=F4)
                     for part in (sums[:, F * LW:F * LW + F4 * P], late[:, :])]
        moved_square = sbuf("moved_square", [P, SQUARED, P])
        ident = sbuf("ident", [P, P])
        top1 = sbuf("top1", [P, 2, N1])
        top1_ctx = sbuf("top1_ctx", [CTX + 1, N1])
        top2 = sbuf("top2", [P, M1, N2])
        top3 = sbuf("top3", [P, M2])
        bias2 = sbuf("bias2", [P, M2])
        dense = sbuf("dense", [P, T, CTX])
        dense_t = sbuf("dense_t", [CTX + 1, T, P])
        inter = late[:, 0:2 * P].rearrange("p (k x) -> p k x", k=2)
        hid1 = late[:, 2 * P:(2 + M1) * P].rearrange("p (m x) -> p m x", m=M1)
        hid2 = late[:, (2 + M1) * P:(2 + M1 + M2) * P].rearrange("p (m x) -> p m x", m=M2)
        y_row = sbuf("y_row", [1, B])

        psum = ctx.enter_context(nc.psum_tensor("psum", [P, 8, BANK], FP32))
        near_bank, far_bank = ([psum[:, 2 * kind + n, :].rearrange("p (s x h) -> p h s x", s=2, h=F)
                                for n in range(2)] for kind in range(2))
        wide_bank = [psum[:, 4 + n, 0:BANK // 2].rearrange("p (x h) -> p h x", h=F) for n in range(2)]

        def by_side(columns, k):
            return columns.rearrange("p h (s x) -> p h s x", s=2)[:, :, :, k * QS:(k + 1) * QS]

        ps_x = psum[:, 6, 0:2 * P].rearrange("p (k x) -> p k x", k=2)
        ps_h1 = psum[:, 7, :].rearrange("p (m x) -> p m x", m=M1)
        ps_h2 = psum[:, 7, 0:M2 * P].rearrange("p (m x) -> p m x", m=M2)
        ps_y = psum[0:1, 7, M2 * P:(M2 + 1) * P]

        last_h1 = [psum[:, bank, m * P:(m + 1) * P] for bank in (7, 0) for m in range(M1 // 2)]
        last_h2 = [psum[:, 1 + m, 0:P] for m in range(M2)]
        last_y = psum[0:1, 3, 0:P]

        def view(flat, start, *dims):
            return bass.AP(flat.tensor, flat.offset + start, [flat.ap[0], *dims])

        def left_at(h, a, c):
            a, c = min(a, c), max(a, c)
            if a < HALF <= c:
                return h * LW + SQ + a * HALF + c - HALF
            if c < HALF:
                return h * LW + a * F4 + c - F4
            return h * LW + SQ + CROSS + HALF + (a - HALF) * F4 + c - HALF - F4

        def others(quarter):
            half = quarter // 2
            return ((4 * half + 1 - quarter) * F4, F4), ((1 - half) * HALF, HALF)

        def near_row(s, quarter, i):
            return (s - 1) * F + quarter * (F4 if s < NEXT else F4 // 2) + i

        ids_loaded = sem("ids_loaded")
        w0_loaded = [sem(f"w0_loaded{n}") for n in range(2)]
        w1_loaded = [sem(f"w1_loaded{n}") for n in range(4)]
        tower_loaded = sem("tower_loaded")
        ident_cleared = sem("ident_cleared")
        ident_ready = sem("ident_ready")
        blocks_cleared = sem("blocks_cleared")
        gathered = [sem(f"gathered{u}") for u in range(4)]
        rows_turned = sem("rows_turned")
        fields_wrapped = sem("fields_wrapped")
        products_ready = sem("products_ready")
        blocks_ready = sem("blocks_ready")
        w0_turned = sem("w0_turned")
        w0_t_saved = sem("w0_t_saved")
        w0_packed = sem("w0_packed")
        dense_loaded = sem("dense_loaded")
        ones_set = sem("ones_set")
        dense_turned = sem("dense_turned")
        dense_saved = sem("dense_saved")
        w_rest_ready = sem("w_rest_ready")
        w0_wrapped = sem("w0_wrapped")
        w_near_ready = sem("w_near_ready")
        near_cleared = sem("near_cleared")
        left_formed = sem("left_formed")
        left_saved = sem("left_saved")
        moved_far_ready = sem("moved_far_ready")
        own_far_added = sem("own_far_added")
        moved_near_ready = sem("moved_near_ready")
        squares_copied = sem("squares_copied")
        moved_square_ready = sem("moved_square_ready")
        v_formed = sem("v_formed")
        v_saved = sem("v_saved")
        v_turned = sem("v_turned")
        v_added = sem("v_added")
        v_square_turned = sem("v_square_turned")
        v_square_saved = sem("v_square_saved")
        quad_formed = sem("quad_formed")
        quad_saved_act = sem("quad_saved_act")
        quad_saved_dve = sem("quad_saved_dve")
        wide_packed = [sem("fields_packed"), sem("squares_packed")]
        last_fields_packed = sem("last_fields_packed")
        pairs_summed = sem("pairs_summed")
        x_summed = sem("x_summed")
        x_saved = sem("x_saved")
        h1_summed = sem("h1_summed")
        h1_ready = sem("h1_ready")
        h2_summed = sem("h2_summed")
        h2_ready = sem("h2_ready")
        y_summed = sem("y_summed")
        y_saved = sem("y_saved")
        y_stored = sem("y_stored")
        block = ctx.enter_context(nc.Block())

        NF, NN = HALF // HPB, F // HPB
        NEAR_BANKS, FAR_BANKS, SQUARE_BANK = (0, 1, 4, 5), (2, 3, 0, 1), 5
        PACKING = (0, F, F4, 0), (F, HALF, SQUARED, F4)
        PACKS = 16 * 2 * P // F, 16 * 2 * P // HALF
        w0_v = w0.rearrange("(r f c) j -> r c f j", r=Q, f=F4)

        EARLY = NN // 2

        def part_groups(n):
            return slice(PARTS[n] * QUAD, (PARTS[n + 1] if n + 1 < NP else NQ) * QUAD)

        def turned_bank(k):
            return 6 + k % 2 if k < EARLY else (0, 2, 4, 1)[k - EARLY]

        def pack(engine, kind, done):
            first, n, width, at = PACKING[kind]
            for r in range(P // n):
                for side in range(2):
                    start = side * SIDE + first
                    engine.dma_start(packed[r * n:(r + 1) * n, at:at + width, side * SIDE:(side + 1) * SIDE],
                                     wide[start:start + n, r * width:(r + 1) * width, :]
                                     ).then_inc(done, 16)

        @block.sync
        def _(sp):
            sp.dma_start(idx[:, :, :], ids.rearrange("p (t f) -> p t f", t=T)).then_inc(ids_loaded, 16)
            for n in range(2):
                part = slice(n * QUAD, (n + 1) * QUAD)
                sp.dma_start(w0_rows[:, part, :], w0.rearrange("(k p) j -> p k j", p=P)[:, part, :]
                             ).then_inc(w0_loaded[n], 16)
            sp.dma_start(dense[:, :, :], dense_ctx.rearrange("(t p) c -> p t c", p=P)).then_inc(dense_loaded, 16)
            w1_v = w1.rearrange("(h m) j -> m h j", m=J)
            for n in range(4):
                part = slice(n * F4, (n + 1) * F4)
                sp.dma_start(w1_sb[:, part, :], w1_v[:, part, :]).then_inc(w1_loaded[n], 16)
            for r in range(Q):
                sp.dma_start(w0_sb[r * F:(r + 1) * F, :, :], w0_v[r]).then_inc(w0_packed, 16)
            with nc.allow_non_contiguous_dma(reason="a few hundred biases"):
                for dst, src in (
                    (top1[:, :, :], w_top1[0:2 * J, :].rearrange("(k p) n -> p k n", p=P)),
                    (top1_ctx[0:CTX, :], w_top1[2 * J:2 * J + CTX, :]),
                    (top1_ctx[CTX:CTX + 1, :], b_top1.unsqueeze(0)),
                    (top2[:, :, :], w_top2.rearrange("(k p) n -> p k n", p=P)),
                    (top3[:, :], w_top3.rearrange("(k p) n -> p (k n)", p=P)),
                    (bias2[:, :], b_top2.rearrange("(k p) -> p k", p=P)),
                ):
                    sp.dma_start(dst, src).then_inc(tower_loaded, 16)

            with sp.Fori(0, T - 1) as t:
                sp.wait_ge(quad_saved_act, t * NQ + NQ)
                pack(sp, 0, wide_packed[0])
                pack(sp, 1, wide_packed[1])
            sp.wait_ge(quad_saved_act, T * NQ)
            pack(sp, 1, wide_packed[1])
            sp.wait_ge(y_saved, T)
            sp.dma_start(out.rearrange("b o -> o b"), y_row[:, :]).then_inc(y_stored, 16)
            sp.wait_ge(y_stored, 16)

        @block.gpsimd
        def _(pool):
            nc.gpsimd.memset(ident[:, :], 0.0).then_inc(ident_cleared, 1)
            pool.wait_ge(ident_cleared, 1)
            nc.gpsimd.affine_select(out=ident[:, :], in_=ident[:, :], compare_op=ALU.not_equal, fill=1.0,
                                    base=0, pattern=[[-1, P]], channel_multiplier=1).then_inc(ident_ready, 1)
            pool.wait_ge(ids_loaded, 16)
            for t in range(T):
                for f in range(F):
                    if t and f % F4 == 0:
                        pool.wait_ge(rows_turned, (t - 1) * 4 + f // F4 + 1)
                    pool.indirect_dma_start(rows[:, f * D:(f + 1) * D], None, tables[f],
                                            bass.IndirectOffsetOnAxis(idx[:, t, f:f + 1], 0)
                                            ).then_inc(gathered[f // F4], 16)
            pool.wait_ge(quad_saved_act, T * NQ)
            pack(pool, 0, last_fields_packed)

        @block.vector
        def _(dve):
            nc.vector.memset(dense_t[:, :, :], 1.0).then_inc(ones_set, 1)

            dve.wait_ge(w0_turned, 2)
            nc.vector.tensor_copy(squares[:, BANK:2 * BANK], psum[:, 1, :]).then_inc(w0_t_saved, 1)
            dve.wait_ge(w0_t_saved, 2)
            swapped = w0_t.rearrange("p a c -> p c a")
            for at, first, second in ((0, (0, F4), (F4, HALF)), (SQ, (0, HALF), (HALF, F)),
                                      (LW - SQ, (HALF, HALF + F4), (HALF + F4, F))):
                a, c = slice(*first), slice(*second)
                n = (a.stop - a.start) * (c.stop - c.start)
                nc.vector.tensor_tensor(w_rest[:, at:at + n].rearrange("p (a c) -> p a c", a=a.stop - a.start),
                                        w0_t[:, a, c], swapped[:, a, c], ALU.add)
            nc.vector.tensor_copy(w_rest[:, SQ + CROSS:SQ + CROSS + HALF],
                                  squares[:, HALF * (F + 1):F * F:F + 1]).then_inc(w_rest_ready, 1)
            nc.vector.tensor_copy(w_near[:, NEAR_PAIRS:NEAR], squares[:, 0:HALF * F:F + 1])
            quarter_step = (F4 * (F + 1), 4)
            for at, n in ((0, F4), (F4, NEXT)):
                last = nc.vector.tensor_tensor(
                    w0_wrap[:, :, :, at:at + n], view(squares[:, :], 0, quarter_step, (F, F4), (1, n)),
                    view(squares[:, :], 0, quarter_step, (1, F4), (F, n)), ALU.add)
            last.then_inc(w0_wrapped, 1)
            dve.wait_ge(w0_wrapped, 1)
            for s in range(1, NEXT + 1):
                n = F4 if s < NEXT else F4 // 2
                start = near_row(s, 0, 0)
                last = nc.vector.tensor_copy(
                    w_near[:, start:start + 4 * n].rearrange("p (u i) -> p u i", u=4),
                    view(squares[:, :], F * F + s, (F4 * WRAP, 4), (WRAP + 1, n)))
            last.then_inc(w_near_ready, 1)
            nc.vector.memset(moved_near[:, :, :], 0.0).then_inc(near_cleared, 1)
            nc.vector.memset(diag_blocks[:, :, :, :], 0.0).then_inc(blocks_cleared, 1)

            left = sums[:, 0:F * LW]

            def left_view(h, a, c, steps):
                here = left_at(h, a, c)
                return view(left, here, *((left_at(h + x, a + y, c + z) - here, n) for (x, y, z), n in steps))

            def form_moved_far(half):
                i, j, c = half * HALF, half * HALF + F4, (1 - half) * HALF
                for n in range(2):
                    dst = moved_far[n][:, :, half * SQ:(half + 1) * SQ].rearrange("p h (i j) -> p h i j", i=F4)
                    last = nc.vector.tensor_tensor(
                        dst,
                        left_view(i, j, c + n * F4, (((0, 0, 1), F4), ((1, 0, 0), F4), ((0, 1, 0), F4))),
                        left_view(j, i, c + n * F4, (((0, 0, 1), F4), ((0, 1, 0), F4), ((1, 0, 0), F4))), ALU.add)
                last.then_inc(moved_far_ready, 1)

            def add_own_far(half):
                dve.wait_ge(moved_far_ready, half + 1)
                i, h = half * HALF, (1 - half) * HALF
                for n in range(2):
                    cols = moved_far[n][:, :, half * SQ:(half + 1) * SQ]
                    last = nc.vector.tensor_tensor(
                        cols, cols, left_view(h + n * F4, i, i + F4, (((1, 0, 0), F4), ((0, 0, 1), SQ))), ALU.add)
                last.then_inc(own_far_added, 1)

            def form_moved_near(quarter):
                for s in range(1, NEXT + 1):
                    runs = ((0, s, F4 - s), (F4 - s, 0, s)) if s < NEXT else ((0, s, s),)
                    for i, j, n in runs:
                        row = near_row(s, quarter, i)
                        i, j = i + quarter * F4, j + quarter * F4
                        for c, nc_ in others(quarter):
                            last = nc.vector.tensor_tensor(
                                moved_near[:, c:c + nc_, row:row + n],
                                left_view(i, j, c, (((0, 0, 1), nc_), ((1, 1, 0), n) if n > 1 else ((0, 0, 0), 1))),
                                left_view(j, i, c, (((0, 0, 1), nc_), ((1, 1, 0), n) if n > 1 else ((0, 0, 0), 1))),
                                ALU.add)
                return last

            def form_moved_near_squares():
                for quarter in range(2):
                    row, i = NEAR_PAIRS + quarter * F4, quarter * F4
                    for c, n in others(quarter):
                        last = nc.vector.tensor_copy(moved_near[:, c:c + n, row:row + F4],
                                                     left_view(i, i, c, (((0, 0, 1), n), ((1, 1, 0), F4))))
                return last

            def turn_rows(t, u):
                dve.wait_ge(gathered[u], (t + 1) * (16 * F4))
                nc.vector.transpose(fields[:, u, 0:F4, :].rearrange("p f g -> p (f g)"),
                                    rows[:, u * F4 * D:(u + 1) * F4 * D]).then_inc(rows_turned, 1)
                dve.wait_ge(rows_turned, t * 4 + u + 1)
                nc.vector.tensor_copy(fields[:, u, F4:WRAP, :], fields[:, u, 0:NEXT, :]).then_inc(fields_wrapped, 1)

            def form_far(gs, half):
                by_group = fields[:, :, :, gs].rearrange("p u f g -> p g u f")
                start = NEAR + half * SQ
                shape = [P, gs.stop - gs.start, F4, F4]
                return nc.vector.tensor_tensor(
                    pairs[:, gs, start:start + SQ].rearrange("p g (i j) -> p g i j", i=F4),
                    by_group[:, :, 2 * half, 0:F4].unsqueeze(3).to_broadcast(shape),
                    by_group[:, :, 2 * half + 1, 0:F4].unsqueeze(2).to_broadcast(shape), ALU.mult)

            def form_first_far():
                for n in range(2):
                    form_far(slice(n * G // 2, (n + 1) * G // 2), 0)

            turn_rows(0, 0)
            turn_rows(0, 1)
            dve.wait_ge(near_cleared, 1)
            dve.wait_ge(left_saved, F // 4)
            form_moved_far(0)
            for quarter in range(2):
                form_moved_near(quarter)
            last = form_moved_near_squares()
            last.then_inc(moved_near_ready, 1)
            dve.wait_ge(left_saved, F // 2 * 3 // 4)
            form_moved_near(2)
            form_first_far()
            turn_rows(0, 2)
            dve.wait_ge(left_saved, F // 2)
            form_moved_far(1)
            add_own_far(0)
            add_own_far(1)
            form_moved_near(3).then_inc(moved_near_ready, 1)
            dve.wait_ge(squares_copied, 1)
            for quarter in (2, 3):
                for h, n in others(quarter):
                    cols = moved_square[:, :, h // SQUARED * HALF:(h + n) // SQUARED * HALF].rearrange(
                        "p f (r i) -> p r f i", i=HALF)[:, :, :, (quarter - 2) * F4:(quarter - 1) * F4]
                    i = quarter * F4
                    last = nc.vector.tensor_tensor(
                        cols, cols, left_view(i, i, h, (((0, 0, SQUARED), n // SQUARED), ((0, 0, 1), SQUARED),
                                                        ((1, 1, 0), F4))), ALU.add)
            last.then_inc(moved_square_ready, 1)

            def add_moved(k):
                dve.wait_ge(v_saved, k + 1)
                dve.wait_ge(v_turned, k + 1)
                v = v_near[:, k * HPB:(k + 1) * HPB, :].rearrange("p h j -> p (h j)")
                nc.vector.tensor_tensor(v, v, psum[:, turned_bank(k), :], ALU.add).then_inc(v_added, 1)

            def form_products(n):
                gs = part_groups(n)
                by_group = fields[:, :, :, gs].rearrange("p u f g -> p g u f")
                for s in range(1, NEXT + 1):
                    size = F4 if s < NEXT else F4 // 2
                    start = near_row(s, 0, 0)
                    nc.vector.tensor_tensor(
                        pairs[:, gs, start:start + 4 * size].rearrange("p g (u i) -> p g u i", u=4),
                        by_group[:, :, :, 0:size], by_group[:, :, :, s:s + size], ALU.mult)
                form_far(gs, 1).then_inc(products_ready, 1)

            def save_quad(t, k):
                dve.wait_ge(quad_formed, t * NQ + k + 1)
                for half in range(2):
                    own = slice(half * SQ, (half + 1) * SQ)
                    last = nc.vector.tensor_copy(by_side(far[own], k),
                                                 far_bank[k % 2][own, (1 - half) * HALF:(2 - half) * HALF])
                last.then_inc(quad_saved_dve, 1)

            turn_rows(0, 3)
            dve.wait_ge(fields_wrapped, 4)
            for n in range(LEAD):
                form_products(n)
            dve.wait_ge(moved_square_ready, 1)
            for k in range(NQ):
                save_quad(0, k)
                if LEAD + k < NP:
                    form_products(LEAD + k)
                if 2 <= k < 2 + EARLY:
                    add_moved(k - 2)
            for n in range(EARLY, NN):
                add_moved(n)
            with dve.Fori(1, T) as t:
                turn_rows(t, 0)
                turn_rows(t, 1)
                form_first_far()
                turn_rows(t, 2)
                turn_rows(t, 3)
                dve.wait_ge(fields_wrapped, (t + 1) * 4)
                for n in range(NP - 1):
                    form_products(n)
                dve.wait_ge(pairs_summed, t)
                for k in range(NQ):
                    save_quad(t, k)
                    if k == 0:
                        form_products(NP - 1)

        @block.scalar
        def _(act):
            def form_near_squares(t):
                act.wait_ge(rows_turned, t * 4 + 2)
                nc.scalar.activation(pairs[:, :, NEAR_PAIRS:NEAR].rearrange("p g (u f) -> p g u f", f=F4),
                                     fields[:, 0:2, 0:F4, :].rearrange("p u f g -> p g u f"), ACT.Square)

            def form_blocks(t, n):
                gs = part_groups(n)
                if n == 0:
                    act.wait_ge(rows_turned, (t + 1) * 4)
                for dst, quarters, fn in ((squares_v[:, gs, F:WIDE], slice(2, 4), ACT.Square),
                                          (squares_v[:, gs, 0:F], slice(0, 4), ACT.Copy)):
                    nc.scalar.activation(dst.rearrange("p g (u f) -> p g u f", f=F4),
                                         fields[:, quarters, 0:F4, gs].rearrange("p u f g -> p g u f"), fn)
                for q in range(Q):
                    own = slice(q * D, (q + 1) * D)
                    last = nc.scalar.copy(diag_blocks[own, gs, q, :].rearrange("p g (u f) -> p g u f", u=4),
                                          fields[own, :, 0:F4, gs].rearrange("p u f g -> p g u f"))
                last.then_inc(blocks_ready, 1)

            act.wait_ge(w0_turned, 1)
            nc.scalar.copy(squares[:, 0:BANK], psum[:, 0, :]).then_inc(w0_t_saved, 1)
            act.wait_ge(dense_turned, 1)
            act.wait_ge(ones_set, 1)
            nc.scalar.copy(dense_t[0:CTX, :, :].rearrange("p t x -> p (t x)"), psum[0:CTX, 7, :]
                           ).then_inc(dense_saved, 1)
            for k in range(F // 2):
                act.wait_ge(left_formed, k + 1)
                b = 2 + 2 * (k % 3)
                nc.scalar.copy(sums[:, 2 * k * LW:2 * (k + 1) * LW].rearrange("p (h w) -> p h w", h=2),
                               psum[:, b:b + 2, 0:LW]).then_inc(left_saved, 1)
                if k == F // 4:
                    form_near_squares(0)
            act.wait_ge(w_near_ready, 1)
            act.wait_ge(left_saved, F // 2)
            last = nc.scalar.copy(moved_square[:, :, :].rearrange("p f (r i) -> p r f i", i=HALF),
                                  view(sums[:, :], SQ + CROSS, (SQUARED * LW, F // SQUARED), (LW, SQUARED),
                                       (1, HALF)))
            last.then_inc(squares_copied, 1)
            for k in range(NN):
                act.wait_ge(v_formed, k + 1)
                nc.scalar.copy(v_near[:, k * HPB:(k + 1) * HPB, :].rearrange("p h j -> p (h j)"),
                               psum[:, NEAR_BANKS[k % 4], :]).then_inc(v_saved, 1)

            def save_quad(t, k):
                act.wait_ge(quad_formed, t * NQ + k + 1)
                nc.scalar.copy(by_side(near, k), near_bank[k % 2])
                for side in range(2):
                    own = slice(side * SIDE, side * SIDE + WIDE)
                    last = nc.scalar.copy(wide[own, :, k * QS:(k + 1) * QS], wide_bank[k % 2][own])
                last.then_inc(quad_saved_act, 1)

            def tower_step(k, t):
                if k == 0:
                    act.wait_ge(h1_summed, t + 1)
                    nc.scalar.activation(hid1, ps_h1, ACT.Relu).then_inc(h1_ready, 1)
                if k == 1:
                    act.wait_ge(h2_summed, t + 1)
                    for m in range(M2):
                        last = nc.scalar.activation(hid2[:, m, :], ps_h2[:, m, :], ACT.Relu,
                                                    bias=bias2[:, m:m + 1])
                    last.then_inc(h2_ready, 1)
                if k == 2:
                    act.wait_ge(y_summed, t + 1)
                    nc.scalar.copy(y_row[:, bass.ds(t * P, P)], ps_y).then_inc(y_saved, 1)

            def save_x(t):
                act.wait_ge(x_summed, t + 1)
                nc.scalar.copy(inter[:, :, :], ps_x).then_inc(x_saved, 1)

            for k in range(NF):
                act.wait_ge(v_formed, NN + k + 1)
                nc.scalar.copy(v_far[:, k * HPB:(k + 1) * HPB, :].rearrange("p h j -> p (h j)"),
                               psum[:, FAR_BANKS[k], :]).then_inc(v_saved, 1)
            act.wait_ge(blocks_cleared, 1)
            for n in range(LEAD):
                form_blocks(0, n)
            act.wait_ge(moved_square_ready, 1)
            for k in range(NQ):
                save_quad(0, k)
                if LEAD + k < NP:
                    form_blocks(0, LEAD + k)
            act.wait_ge(v_square_turned, 1)
            nc.scalar.copy(v_square[:, :, :].rearrange("p h j -> p (h j)"), psum[:, SQUARE_BANK, :]
                           ).then_inc(v_square_saved, 1)
            form_near_squares(1)
            for n in range(NP - 1):
                form_blocks(1, n)
            act.wait_ge(tower_loaded, 16 * 6)

            def save_quads(t):
                act.wait_ge(pairs_summed, t)
                for kind in range(2):
                    act.wait_ge(wide_packed[kind], t * PACKS[kind])
                for k in range(NQ):
                    save_quad(t, k)
                    if k == 0:
                        form_blocks(t, NP - 1)
                    if k == 1:
                        save_x(t - 1)

            with act.Fori(1, T - 1) as t:
                save_quads(t)
                tower_step(0, t - 1)
                form_near_squares(t + 1)
                form_blocks(t + 1, 0)
                form_blocks(t + 1, 1)
                tower_step(1, t - 1)
                for n in range(2, NP - 1):
                    form_blocks(t + 1, n)
                tower_step(2, t - 1)
            save_quads(T - 1)
            for k in range(3):
                tower_step(k, T - 2)
            save_x(T - 1)
            for half in range(2):
                act.wait_ge(h1_summed, T + half)
                m = half * M1 // 2
                nc.scalar.activation(hid1[:, m:m + M1 // 2, :],
                                     psum[:, (7, 0)[half], 0:M1 // 2 * P].rearrange("p (m x) -> p m x", x=P),
                                     ACT.Relu).then_inc(h1_ready, 1)
            for m in range(M2):
                act.wait_ge(h2_summed, T + m)
                nc.scalar.activation(hid2[:, m, :], last_h2[m], ACT.Relu, bias=bias2[:, m:m + 1]
                                     ).then_inc(h2_ready, 1)
            act.wait_ge(y_summed, T)
            nc.scalar.copy(y_row[:, (T - 1) * P:T * P], last_y).then_inc(y_saved, 1)

        @block.tensor
        def _(pe):
            def mm(*args, **kw):
                return nc.tensor.matmul(*args, **kw)

            pe.wait_ge(ident_ready, 1)
            for n in range(2):
                pe.wait_ge(w0_loaded[n], 16)
                for k in range(QUAD):
                    last = nc.tensor.transpose(psum[:, n, k * P:(k + 1) * P], w0_rows[:, n * QUAD + k, :],
                                               ident[:, :])
                last.then_inc(w0_turned, 1)
            pe.wait_ge(dense_loaded, 16)
            for t in range(T):
                last = nc.tensor.transpose(psum[0:CTX, 7, t * P:(t + 1) * P], dense[:, t, :], ident[:, :])
            last.then_inc(dense_turned, 1)

            pe.wait_ge(w_rest_ready, 1)
            for k in range(F // 2):
                if 2 * k % F4 == 0:
                    pe.wait_ge(w1_loaded[2 * k // F4], 16)
                if k >= 3:
                    pe.wait_ge(left_saved, k - 2)
                if k == 2:
                    pe.wait_ge(dense_saved, 1)
                for n in range(2):
                    last = mm(psum[:, 2 + 2 * (k % 3) + n, 0:LW], w1_sb[:, 2 * k + n, :],
                              w_rest[:, :], start=True, stop=True)
                last.then_inc(left_formed, 1)

            pe.wait_ge(w_near_ready, 1)
            for k in range(NN):
                if k == 2:
                    pe.wait_ge(left_saved, F // 2 - 2)
                if k >= 4:
                    pe.wait_ge(v_saved, k - 3)
                mm(psum[:, NEAR_BANKS[k % 4], :], w_near[:, :], w1_sb[:, k * HPB:(k + 1) * HPB, :],
                   start=True, stop=True).then_inc(v_formed, 1)
            pe.wait_ge(left_saved, F // 2)

            def turn_near(k):
                if 2 <= k < EARLY:
                    pe.wait_ge(v_added, k - 1)
                for n in range(HPB):
                    last = nc.tensor.transpose(psum[:, turned_bank(k), n * J:(n + 1) * J],
                                               moved_near[:, k * HPB + n, :], ident[:, :])
                last.then_inc(v_turned, 1)

            def turn_far(k):
                if k == 0:
                    pe.wait_ge(own_far_added, 2)
                if FAR_BANKS[k] in NEAR_BANKS:
                    pe.wait_ge(v_saved, NN)
                for n in range(HPB):
                    h = k * HPB + n
                    last = nc.tensor.transpose(psum[:, FAR_BANKS[k], n * J:(n + 1) * J],
                                               moved_far[h // F4][:, h % F4, :], ident[:, :])
                last.then_inc(v_formed, 1)

            def turn_squares():
                pe.wait_ge(moved_square_ready, 1)
                for f in range(SQUARED):
                    last = nc.tensor.transpose(psum[:, SQUARE_BANK, f * J:(f + 1) * J], moved_square[:, f, :],
                                               ident[:, :])
                last.then_inc(v_square_turned, 1)

            def form_quad(t, k, first=False):
                if k in PARTS:
                    pe.wait_ge(blocks_ready, t * NP + PARTS.index(k) + 1)
                    pe.wait_ge(products_ready, t * NP + PARTS.index(k) + 1)
                if not first:
                    pe.wait_ge(quad_saved_act, t * NQ + k - 1)
                    pe.wait_ge(quad_saved_dve, t * NQ + k - 1)
                blocks = diag_blocks[:, k * QUAD:(k + 1) * QUAD, :, :].rearrange("p g q h -> p g (q h)")

                def form_pair_sums():
                    for n in range(QUAD):
                        g, columns = k * QUAD + n, slice(n * P, (n + 1) * P)
                        mm(psum[:, k % 2, columns], pairs[:, g, 0:NEAR], blocks[:, n, :], start=True, stop=True)
                        last = mm(psum[:, 2 + k % 2, columns], pairs[:, g, NEAR:PAIRS], blocks[:, n, :],
                                  start=True, stop=True)
                    return last

                def form_wide_sums():
                    for n in range(QUAD // 2):
                        for side in range(2):
                            g = side * QUAD // 2 + n
                            last = mm(psum[side * SIDE:side * SIDE + WIDE, 4 + k % 2, n * P:(n + 1) * P],
                                      squares_v[:, k * QUAD + g, :], blocks[:, g, :], start=True, stop=True)
                    return last

                if k % 2 == 0:
                    form_pair_sums()
                    form_wide_sums().then_inc(quad_formed, 1)
                else:
                    form_wide_sums()
                    form_pair_sums().then_inc(quad_formed, 1)

            def form_x1(t, last):
                if last:
                    pe.wait_ge(last_fields_packed, PACKS[0])
                else:
                    pe.wait_ge(wide_packed[0], (t + 1) * PACKS[0])
                for f in range(F4):
                    mm(ps_x[:, 0, :], w0_sb[:, f, :], packed[:, f, :], start=False, stop=f == F4 - 1,
                       skip_group_check=True)

            def tower_step(k, t):
                if k == 0:
                    for m in range(M1):
                        mm(ps_h1[:, m, :], top1_ctx[:, m * P:(m + 1) * P], dense_t[:, bass.ds(t, 1), :],
                           start=m == 0, stop=False, skip_group_check=True)
                    pe.wait_ge(x_saved, t + 1)
                    for m in range(M1):
                        for i in range(2):
                            last = mm(ps_h1[:, m, :], top1[:, i, m * P:(m + 1) * P], inter[:, i, :],
                                      start=False, stop=i == 1, skip_group_check=True)
                    last.then_inc(h1_summed, 1)
                if k == 1:
                    pe.wait_ge(h1_ready, t + 1)
                    for m in range(M2):
                        for i in range(M1):
                            last = mm(ps_h2[:, m, :], top2[:, i, m * P:(m + 1) * P], hid1[:, i, :],
                                      start=i == 0, stop=i == M1 - 1)
                    last.then_inc(h2_summed, 1)
                if k == 2:
                    pe.wait_ge(h2_ready, t + 1)
                    for i in range(M2):
                        last = mm(ps_y, top3[:, i:i + 1], hid2[:, i, :], start=i == 0, stop=i == M2 - 1)
                    last.then_inc(y_summed, 1)

            def contract(t, first=False, last=False):
                if not first:
                    tower_step(0, t - 1)
                else:
                    pe.wait_ge(quad_saved_act, NQ - 1)
                    pe.wait_ge(quad_saved_dve, NQ - 1)
                    turn_near(EARLY)
                    turn_near(EARLY + 1)
                    turn_near(EARLY + 2)
                pe.wait_ge(quad_saved_act, (t + 1) * NQ)
                pe.wait_ge(quad_saved_dve, (t + 1) * NQ)
                if first:
                    pe.wait_ge(w0_packed, 16 * Q)
                    turn_near(EARLY + 3)
                    turn_squares()
                for h in range(F):
                    if first and h % HPB == 0:
                        pe.wait_ge(v_added, h // HPB + 1)
                    mm(ps_x[:, 1, :], v_near[:, h, :], near[:, h, :], start=h == 0, stop=False)
                if not first:
                    tower_step(1, t - 1)
                for h in range(HALF):
                    far_part = mm(ps_x[:, 1, :], v_far[:, h, :], far[:, h, :], start=False, stop=False)
                far_part.then_inc(pairs_summed, 1)
                if not first:
                    tower_step(2, t - 1)
                form_x1(t, last)
                if first:
                    pe.wait_ge(v_square_saved, 1)

            def finish_x2(t):
                pe.wait_ge(wide_packed[1], (t + 1) * PACKS[1])
                for f in range(SQUARED):
                    final = mm(ps_x[:, 1, :], v_square[:, f, :], packed[:, F4 + f, :], start=False,
                               stop=f == SQUARED - 1)
                final.then_inc(x_summed, 1)

            pe.wait_ge(tower_loaded, 16 * 6)
            for k in range(NF):
                turn_far(k)
            pe.wait_ge(moved_near_ready, 2)
            turn_near(0)
            turn_near(1)
            pe.wait_ge(v_saved, NN + NF)
            for k in range(NQ):
                form_quad(0, k, first=k < 2)
                if 2 <= k - 1 < EARLY:
                    turn_near(k - 1)
            contract(0, first=True)

            def form_quads(t):
                for k in range(NQ):
                    form_quad(t, k)
                    if k == 1:
                        finish_x2(t - 1)

            with pe.Fori(1, T - 1) as t:
                form_quads(t)
                contract(t)
            form_quads(T - 1)
            contract(T - 1, last=True)
            finish_x2(T - 1)
            pe.wait_ge(y_saved, T - 1)
            for m in range(M1):
                mm(last_h1[m], top1_ctx[:, m * P:(m + 1) * P], dense_t[:, T - 1, :],
                   start=m % (M1 // 2) == 0, stop=False, skip_group_check=True)
            pe.wait_ge(x_saved, T)
            for m in range(M1):
                for i in range(2):
                    last = mm(last_h1[m], top1[:, i, m * P:(m + 1) * P], inter[:, i, :],
                              start=False, stop=i == 1, skip_group_check=True)
                if (m + 1) % (M1 // 2) == 0:
                    last.then_inc(h1_summed, 1)
            for i in range(M1):
                if i % (M1 // 2) == 0:
                    pe.wait_ge(h1_ready, T + i // (M1 // 2))
                for m in range(M2):
                    last = mm(last_h2[m], top2[:, i, m * P:(m + 1) * P], hid1[:, i, :],
                              start=i == 0, stop=i == M1 - 1)
                    if i == M1 - 1:
                        last.then_inc(h2_summed, 1)
            for i in range(M2):
                pe.wait_ge(h2_ready, T + i)
                last = mm(last_y, top3[:, i:i + 1], hid2[:, i, :], start=i == 0, stop=i == M2 - 1)
            last.then_inc(y_summed, 1)


def kernel(**inputs):
    import numpy as np
    import concourse.bacc as bacc
    from concourse.bass_utils import run_bass_kernel_spmd

    nc = bacc.Bacc("TRN2", target_bir_lowering=False, num_devices=1)
    arrays = {}

    def dram(name):
        a = np.ascontiguousarray(inputs[name])
        arrays["in_" + name] = a
        return nc.dram_tensor("in_" + name, a.shape, mybir.dt.from_np(a.dtype), kind="ExternalInput").ap()

    ids = inputs["ids"].reshape(T, 2, NQ, QUAD // 2, Q, F).transpose(4, 2, 1, 3, 0, 5).reshape(P, T * F)
    inputs = {**inputs, "ids": ids}
    tables = [dram(f"tbl_{f}") for f in range(F)]
    args = {name: dram(name) for name in ("dense_ctx", "ids", "W_top1", "b_top1", "W_top2", "b_top2", "W_top3",
                                          "L0_rec_W0", "L0_rec_W1")}
    out = nc.dram_tensor("out", (B, 1), FP32, kind="ExternalOutput").ap()
    build(nc, args["dense_ctx"], args["ids"], tables, args["W_top1"], args["b_top1"], args["W_top2"],
          args["b_top2"], args["W_top3"], args["L0_rec_W0"], args["L0_rec_W1"], out)
    result = run_bass_kernel_spmd(nc, [arrays], core_ids=[0])
    return result.results[0]["out"]
```
